# Optimizing a Trainium2 kernel written in Bass

```python
import numpy as np
import jax
import jax.numpy as jnp

def _softmax(x, axis=-1):
    return jax.nn.softmax(x, axis=axis)

def _gelu(x):
    return jax.nn.gelu(x, approximate=True)

def _silu(x):
    return jax.nn.silu(x)

def _sigmoid(x):
    return jax.nn.sigmoid(x)

def _layernorm(x, axis=-1, eps=1e-05):
    m = jnp.mean(x, axis=axis, keepdims=True)
    v = jnp.var(x, axis=axis, keepdims=True)
    return (x - m) / jnp.sqrt(v + eps)

def _scatter_add(tgt, idx, src, axis=0):
    return tgt.at[idx].add(src)

def _segment_sum(src, seg, n):
    return jax.ops.segment_sum(src, seg, n)
kernel_name = 'mk_prb_d2_jaxref_r8_95a273'

def setup_inputs(seed: int=0):
    np.random.seed(seed)
    _w = jnp.asarray

    def _L0_attn_setup():
        import jax, jax.numpy as jnp
        import numpy as np
        B, T, C = (8, 128, 256)

        def wkv(time_decay, time_first, k, v):
            w = -jnp.exp(time_decay)
            u = time_first
            b, t, c = k.shape
            k_t = jnp.transpose(k, (1, 0, 2))
            v_t = jnp.transpose(v, (1, 0, 2))

            def step(carry, kv):
                p, q, o = carry
                kt, vt = kv
                no = jnp.maximum(o, u + kt)
                A = jnp.exp(o - no)
                Bc = jnp.exp(u + kt - no)
                y = (A * p + Bc * vt) / (A * q + Bc)
                no2 = jnp.maximum(w + o, kt)
                A2 = jnp.exp(w + o - no2)
                B2 = jnp.exp(kt - no2)
                return ((A2 * p + B2 * vt, A2 * q + B2, no2), y)
            init = (jnp.zeros((b, c), k.dtype), jnp.zeros((b, c), k.dtype), jnp.full((b, c), -1e+38, k.dtype))
            _, y = jax.lax.scan(step, init, (k_t, v_t))
            return jnp.transpose(y, (1, 0, 2))
        key = jax.random.key(seed)
        k1, k2, k3, k4, k5 = jax.random.split(key, 5)
        x = jax.random.normal(k1, (B, T, C), dtype=jnp.float32)
        W_rvk = jax.random.normal(k2, (3 * C, C), dtype=jnp.float32) / np.sqrt(C).astype(np.float32)
        W_out = jax.random.normal(k3, (C, C), dtype=jnp.float32) / np.sqrt(C).astype(np.float32)
        time_decay = jax.random.normal(k4, (C,), dtype=jnp.float32) * 0.1
        time_first = jax.random.normal(k5, (C,), dtype=jnp.float32) * 0.1
        return {'x': x, 'W_rvk': W_rvk, 'W_out': W_out, 'time_decay': time_decay, 'time_first': time_first}
    _L0_attn_in = _L0_attn_setup()

    def _L0_ffn_setup():
        import jax, jax.numpy as jnp
        import numpy as np
        D_MODEL = 256
        D_FF = 1024
        N_EXPERTS = 4
        B, S = (2, 256)
        key = jax.random.key(seed)
        ks = jax.random.split(key, 6)
        scale = 0.02
        return {'hidden_states': jax.random.normal(ks[0], (B, S, D_MODEL), dtype=jnp.float32), 'Wr': jax.random.normal(ks[1], (D_MODEL, N_EXPERTS), dtype=jnp.float32) * scale, 'br': jnp.zeros((N_EXPERTS,), dtype=jnp.float32), 'Wg': jax.random.normal(ks[2], (N_EXPERTS, D_MODEL, D_FF), dtype=jnp.float32) * scale, 'Wu': jax.random.normal(ks[3], (N_EXPERTS, D_MODEL, D_FF), dtype=jnp.float32) * scale, 'Wd': jax.random.normal(ks[4], (N_EXPERTS, D_FF, D_MODEL), dtype=jnp.float32) * scale}
    _L0_ffn_in = _L0_ffn_setup()

    def _L1_attn_setup():
        import jax, jax.numpy as jnp
        import numpy as np
        key = jax.random.key(seed)
        k1, k2, k3, k4 = jax.random.split(key, 4)
        batch, n_channels, t = (4, 256, 256)
        n_blocks, block_size, ks = (128, 64, 16)
        n_block_row = n_channels // block_size
        x = jax.random.normal(k1, (batch, n_channels, t), dtype=jnp.float32)
        block_values = jax.random.normal(k2, (n_blocks, block_size, block_size, ks), dtype=jnp.float32) * 0.05
        cols = jax.random.randint(k3, (n_blocks,), 0, n_block_row, dtype=jnp.int32)
        rows = jax.random.randint(k4, (n_blocks,), 0, n_block_row, dtype=jnp.int32)
        return {'x': x, 'block_values': block_values, 'cols': cols, 'rows': rows}
    _L1_attn_in = _L1_attn_setup()

    def _L1_ffn_setup():
        import jax, jax.numpy as jnp
        import numpy as np

        def ternary_quantize(t, threshold, scale):
            return jnp.where(t > threshold, scale, jnp.where(t < -threshold, -scale, 0.0)).astype(t.dtype)
        key = jax.random.key(seed)
        k1, k2, k3 = jax.random.split(key, 3)
        B, S, D = (4, 512, 256)
        x = jax.random.normal(k1, (B, S, D), dtype=jnp.float32)
        weight = jax.random.normal(k2, (D, D), dtype=jnp.float32) * 0.02
        rram_variation = jax.random.normal(k3, (D, D), dtype=jnp.float32) * 0.05
        return {'x': x, 'weight': weight, 'rram_variation': rram_variation}
    _L1_ffn_in = _L1_ffn_setup()
    _d = {'L0_attn_x': _L0_attn_in['x'], 'L0_attn_W_rvk': _L0_attn_in['W_rvk'], 'L0_attn_W_out': _L0_attn_in['W_out'], 'L0_attn_time_decay': _L0_attn_in['time_decay'], 'L0_attn_time_first': _L0_attn_in['time_first'], 'L0_ffn_Wr': _L0_ffn_in['Wr'], 'L0_ffn_br': _L0_ffn_in['br'], 'L0_ffn_Wg': _L0_ffn_in['Wg'], 'L0_ffn_Wu': _L0_ffn_in['Wu'], 'L0_ffn_Wd': _L0_ffn_in['Wd'], 'L1_attn_block_values': _L1_attn_in['block_values'], 'L1_attn_cols': _L1_attn_in['cols'], 'L1_attn_rows': _L1_attn_in['rows'], 'L1_ffn_weight': _L1_ffn_in['weight'], 'L1_ffn_rram_variation': _L1_ffn_in['rram_variation']}
    _x0 = _d['L0_attn_x']
    _d['L0_attn_x'] = jax.random.normal(jax.random.fold_in(jax.random.key(seed), 1), (2, 1024, 256), dtype=_x0.dtype)
    del _x0
    return _d

def reference(L0_attn_x, L0_attn_W_rvk, L0_attn_W_out, L0_attn_time_decay, L0_attn_time_first, L0_ffn_Wr, L0_ffn_br, L0_ffn_Wg, L0_ffn_Wu, L0_ffn_Wd, L1_attn_block_values, L1_attn_cols, L1_attn_rows, L1_ffn_weight, L1_ffn_rram_variation):

    def _L0_attn_ref(x, W_rvk, W_out, time_decay, time_first):
        import jax, jax.numpy as jnp
        import numpy as np
        B, T, C = (8, 128, 256)

        def wkv(time_decay, time_first, k, v):
            w = -jnp.exp(time_decay)
            u = time_first
            b, t, c = k.shape
            k_t = jnp.transpose(k, (1, 0, 2))
            v_t = jnp.transpose(v, (1, 0, 2))

            def step(carry, kv):
                p, q, o = carry
                kt, vt = kv
                no = jnp.maximum(o, u + kt)
                A = jnp.exp(o - no)
                Bc = jnp.exp(u + kt - no)
                y = (A * p + Bc * vt) / (A * q + Bc)
                no2 = jnp.maximum(w + o, kt)
                A2 = jnp.exp(w + o - no2)
                B2 = jnp.exp(kt - no2)
                return ((A2 * p + B2 * vt, A2 * q + B2, no2), y)
            init = (jnp.zeros((b, c), k.dtype), jnp.zeros((b, c), k.dtype), jnp.full((b, c), -1e+38, k.dtype))
            _, y = jax.lax.scan(step, init, (k_t, v_t))
            return jnp.transpose(y, (1, 0, 2))
        rvk = jnp.einsum('btc,dc->btd', x, W_rvk)
        r, v, k = jnp.split(rvk, 3, axis=-1)
        y = jax.nn.sigmoid(r) * wkv(time_decay, time_first, k, v)
        return jnp.einsum('btc,dc->btd', y, W_out)

    def _L0_ffn_ref(hidden_states, Wr, br, Wg, Wu, Wd):
        import jax, jax.numpy as jnp
        import numpy as np
        D_MODEL = 256
        D_FF = 1024
        N_EXPERTS = 4
        B, S = (2, 256)
        b, s, d = hidden_states.shape
        x = hidden_states.reshape(-1, d)
        logits = x @ Wr + br
        probs = jax.nn.softmax(logits, axis=-1)
        top_w, top_idx = jax.lax.top_k(probs, 1)
        g = jnp.einsum('td,edf->tef', x, Wg)
        u = jnp.einsum('td,edf->tef', x, Wu)
        h = jax.nn.silu(g) * u
        y = jnp.einsum('tef,efd->ted', h, Wd)
        sel = jnp.take_along_axis(y, top_idx[:, :, None], axis=1)[:, 0]
        out = sel * top_w
        return out.reshape(b, s, d)

    def _L1_attn_ref(x, block_values, cols, rows):
        import jax, jax.numpy as jnp
        import numpy as np
        batch, n_channels, t = x.shape
        n_blocks, bs, _, ks = block_values.shape
        n_block_row = -(-n_channels // bs)
        pad = n_block_row * bs - n_channels
        if pad > 0:
            x = jnp.pad(x, ((0, 0), (0, pad), (0, 0)))
        xb = x.reshape(batch, n_block_row, bs, t)
        x_unfold = xb[:, cols].reshape(batch, n_blocks * bs, t)
        W = block_values.reshape(n_blocks * bs, bs, ks)
        o = jax.lax.conv_general_dilated(x_unfold, W, window_strides=(1,), padding=[(ks - 1, 0)], dimension_numbers=('NCH', 'OIH', 'NCH'), feature_group_count=n_blocks)
        o = o.reshape(batch, n_blocks, bs, t)
        y = jnp.zeros((batch, n_block_row, bs, t), o.dtype).at[:, rows].add(o)
        y = y.reshape(batch, n_block_row * bs, t)
        return y[:, :n_channels, :]

    def _L1_ffn_ref(x, weight, rram_variation):
        import jax, jax.numpy as jnp
        import numpy as np

        def ternary_quantize(t, threshold, scale):
            return jnp.where(t > threshold, scale, jnp.where(t < -threshold, -scale, 0.0)).astype(t.dtype)
        TH_X, SC_X = (0.33, 0.5)
        TH_W, SC_W = (0.2, 0.6)
        x_q = ternary_quantize(x, TH_X, SC_X)
        w_q = ternary_quantize(weight, TH_W, SC_W)
        w_rram = w_q + rram_variation
        return jnp.einsum('bsd,od->bso', x_q, w_rram)
    x = L0_attn_x
    xn = _layernorm(x, axis=-1)
    x = x + _L0_attn_ref(xn, L0_attn_W_rvk, L0_attn_W_out, L0_attn_time_decay, L0_attn_time_first) + _L0_ffn_ref(xn, L0_ffn_Wr, L0_ffn_br, L0_ffn_Wg, L0_ffn_Wu, L0_ffn_Wd)
    xn = _layernorm(x, axis=-1)
    x = x + _L1_attn_ref(xn, L1_attn_block_values, L1_attn_cols, L1_attn_rows) + _L1_ffn_ref(xn, L1_ffn_weight, L1_ffn_rram_variation)
    return x

_drawn_inputs = setup_inputs


def setup_inputs(seed=0):
    import zlib

    import numpy as np

    out = dict(_drawn_inputs(seed))
    spreads = {'L0_ffn_br': (0.0, 0.8)}
    factors = {'L0_attn_time_decay': 3.544,
     'L0_attn_time_first': 4.308,
     'L0_ffn_Wr': 5.293,
     'L0_ffn_Wg': 4.446,
     'L0_ffn_Wu': 4.409,
     'L0_ffn_Wd': 4.425}
    for name, (base, spread) in spreads.items():
        noise = np.random.default_rng([zlib.crc32(name.encode()), seed]).standard_normal(out[name].shape)
        drawn = base * np.exp(spread * noise) if base else spread * noise
        out[name] = jnp.asarray(drawn.astype(out[name].dtype))
    for name, factor in factors.items():
        out[name] = (out[name] * factor).astype(out[name].dtype)
    return out
```

```python
from contextlib import ExitStack

import numpy as np

import concourse.bass as bass
from concourse import mybir

F32 = mybir.dt.float32
I32 = mybir.dt.int32
ALU = mybir.AluOpType
ACT = mybir.ActivationFunctionType
AX = mybir.AxisListType
ds = bass.ds

P = 128
BATCH, SEQ, C = 2, 1024, 256
NT = BATCH * SEQ // P
KC = C // P
NE, FF = 4, 1024
KF = FF // P
MT = NT + NE - 1
LOADS = MT + 2
QT = 512
ROUNDS = BATCH * SEQ // QT
NBLK, BS, KS = 128, 64, 16
NROW = SEQ // BS
TAPS = KS // 2
SPAN = C + TAPS
XW = C + KS
SLOTS = 16
BW = KS * BS // 2
RING = 3
TH_X, TH_W, SC_W = 0.33, 0.2, 0.6
EPS = 1e-5
UNIT = 19
RP = 6


def col_of(i):
    b, half, m = i // 8, (i % 8) // 4, i % 4
    return (2 * half + b) * QT + m * P


def build(nc, x, w_rvk, w_out, decay, first, w_r, b_r, w_g, w_u, w_d, blocks, cols, rows, w_t, rram, out):
    x_v = x.rearrange("(i p) c -> p i c", p=P)
    out_v = out.rearrange("(i p) c -> p i c", p=P)
    slots_x = nc.dram_tensor("slots_x", (LOADS * P, C), F32).ap()
    slots_y = nc.dram_tensor("slots_y", (MT * P, C), F32).ap()

    with ExitStack() as ctx:
        def sb(name, shape, dt=F32):
            return ctx.enter_context(nc.sbuf_tensor(name, shape, dt))

        def bank(name):
            return ctx.enter_context(nc.psum_tensor(name, [P, 512], F32))

        def sem(name):
            return ctx.enter_context(nc.semaphore(name))

        big = sb("big", [P, NE * 3 * KC * FF])
        per_w = NE * KC * FF
        wg = big[:, 0:per_w].rearrange("p (e k f) -> p e k f", e=NE, k=KC)
        wu = big[:, per_w:2 * per_w].rearrange("p (e k f) -> p e k f", e=NE, k=KC)
        wd = big[:, 2 * per_w:3 * per_w].rearrange("p (e k c) -> p e k c", e=NE, k=KF)
        at = 0

        def part(cols_):
            nonlocal at
            at += cols_
            assert at <= NE * 3 * KC * FF
            return big[:, at - cols_:at]

        xc = part(BATCH * NROW * XW).rearrange("p (b r u) -> p b r u", b=BATCH, r=NROW)
        z = part(NROW * BATCH * SPAN).rearrange("p (r b s) -> p r b s", r=NROW, b=BATCH)
        yg = part(NT * C).rearrange("p (i c) -> p i c", i=NT)
        xln = part(4 * C).rearrange("p (m c) -> p m c", m=4)
        xq = part(4 * C).rearrange("p (m c) -> p m c", m=4)

        tr = sb("tr", [P, KC, NT * P])
        acc = sb("acc", [P, (SLOTS + 1) * BW])
        x_in = acc[:, 0:NT * C].rearrange("p (i c) -> p i c", i=NT)
        xn = acc[:, NT * C:2 * NT * C].rearrange("p (i c) -> p i c", i=NT)
        accs = acc[:, :].rearrange("p (g w) -> p g w", w=BW)
        ring = sb("ring", [P, RING, BW])
        wk = sb("wk", [P, 6 * QT + 3 * (QT + 1) + 3 * QT])
        kvr = wk[:, 0:6 * QT].rearrange("p (c a t) -> p c a t", c=KC, a=3)
        opq = wk[:, 6 * QT:6 * QT + 3 * (QT + 1)].rearrange("p (a t) -> p a t", a=3)
        o0 = 6 * QT + 3 * (QT + 1)
        b1, b2, b3 = (wk[:, o0 + n * QT:o0 + (n + 1) * QT] for n in range(3))
        x1 = wk[:, 0:NT * C].rearrange("p (i c) -> p i c", i=NT)
        o1 = NT * C
        wout_sb = wk[:, o1:o1 + KC * C].rearrange("p (k c) -> p k c", k=KC)
        wt_sb = wk[:, o1 + 512:o1 + 1024].rearrange("p (k c) -> p k c", k=KC)
        rr_sb = wk[:, o1 + 1024:o1 + 1536].rearrange("p (k c) -> p k c", k=KC)
        h = sb("h", [P, FF])
        th = sb("th", [P, 2, 512])
        h_t = sb("h_t", [P, KF, P])
        y_sb = sb("y_sb", [P, 2, C])
        xs = sb("xs", [P, C])
        xs_t = sb("xs_t", [P, 2, KC, P])
        wrvk_sb = sb("wrvk_sb", [P, KC, 3 * C])
        wr_sb = sb("wr_sb", [P, KC, NE])
        br_sb = sb("br_sb", [P, NE])
        dec = sb("dec", [P, KC])
        wv = sb("wv", [P, KC])
        uv = sb("uv", [P, KC])
        carry = sb("carry", [P, KC, ROUNDS + 2, 3])
        ident = sb("ident", [P, P])
        before = sb("before", [P, P])
        after = h[:, 0:P]
        zero = h[:, P:P + C]
        iota = h_t[:, 0, :]
        iota_r = h_t[:, 1, :]
        ones = sb("ones", [P, P])
        starts = sb("starts", [P, NT])
        tiles = sb("tiles", [P, LOADS])
        rows_i = sb("rows_i", [P, NBLK], I32)
        cols_i = sb("cols_i", [P, NBLK], I32)
        rc_i = sb("rc_i", [P, 2], I32)
        slot_i = sb("slot_i", [P, NBLK], I32)
        spill = sb("spill", [P, NBLK])
        srow_i = sb("srow_i", [P, SLOTS], I32)
        scol_i = sb("scol_i", [P, SLOTS], I32)
        pairs_i = sb("pairs_i", [P, 1], I32)
        pos_i = sb("pos_i", [P, NT], I32)
        eid_i = sb("eid_i", [P, LOADS], I32)
        top_w = sb("top_w", [P, NT])
        stats = sb("stats", [P, NT, 6])
        mv = sb("mv", [P, NT, 2])
        ve = sb("ve", [P, NT])
        rstd = sb("rstd", [P, NT])
        lg = b1[:, 0:64].rearrange("p (i e) -> p i e", e=NE)
        mx = b1[:, 64:80]
        oh = b1[:, 80:144].rearrange("p (i e) -> p i e", e=NE)
        eq = b1[:, 144:208].rearrange("p (i e) -> p i e", e=NE)
        seen = b1[:, 208:224]
        ex = b1[:, 224:288].rearrange("p (i e) -> p i e", e=NE)
        sums = b1[:, 288:304]
        incl = b1[:, 304:368].rearrange("p (e i) -> p e i", e=NE)
        cmp = b1[:, 368:432].rearrange("p (e i) -> p e i", e=NE)
        t_e = b1[:, 432:436]
        t_end = b1[:, 436:440]
        t_beg = b1[:, 440:444]
        ps = b1[:, 444:508].rearrange("p (i e) -> p i e", e=NE)
        pos = b2[:, 0:16]
        ecmp = b2[:, 16:16 + 3 * LOADS].rearrange("p (s e) -> p s e", e=3)
        eid = b2[:, 80:80 + LOADS]
        key = b2[:, 128:256]
        same = b2[:, 256:384]
        tmp = b2[:, 384:512]
        first_b = b3[:, 0:128]
        gid_d = b3[:, 128:256]
        row_b = b3[:, 256:384]
        col_b = b3[:, 384:512]
        sel = opq[:, 0, 0:SLOTS]
        sm = opq[:, 1, 0:16]
        keyc, seenc, firstc, fidx, gid, rowf, colf = (sm[:, n:n + 1] for n in range(7))
        wbuf = h[:, :].rearrange("p (n w) -> p n w", n=2)
        spare = th[:, 0, :]
        shifted = h_t[:, :, :].rearrange("p k n -> p (k n)").rearrange("p (n b c) -> p n b c", n=2, b=BATCH)
        res = ring[:, 0:2, :].rearrange("p n (b c) -> p n b c", b=BATCH)

        pg = [bank("pg0"), bank("pg1")]
        pu = [bank("pu0"), bank("pu1")]
        pt = [bank("pt0"), bank("pt1")]
        py = bank("py")
        pr = bank("pr")
        four = [pg[0], pu[0], pg[1], pu[1]]
        six = four + pt
        dense_bank = pu + [py, pr]
        s_x = [sem(f"s_x{n}") for n in range(4)]
        s_c = sem("s_c")
        s_zf = sem("s_zf")
        s_we = [sem(f"s_we{n}") for n in range(NE)]
        s_wt = sem("s_wt")
        s_k = sem("s_k")
        s_p = sem("s_p")
        s_ve = sem("s_ve")
        s_sd = sem("s_sd")
        s_xn = sem("s_xn")
        s_tp = sem("s_tp")
        s_ta = sem("s_ta")
        s_tv = sem("s_tv")
        s_lg = sem("s_lg")
        s_sub = sem("s_sub")
        s_el = sem("s_el")
        s_oh = sem("s_oh")
        s_cn = sem("s_cn")
        s_pos = sem("s_pos")
        s_fb = sem("s_fb")
        s_gp = sem("s_gp")
        s_gd = sem("s_gd")
        s_gt = sem("s_gt")
        s_cv = sem("s_cv")
        s_sc = sem("s_sc")
        s_bk = [sem(f"s_bk{n}") for n in range(RING)]
        s_ba = sem("s_ba")
        s_xs = sem("s_xs")
        s_xt = sem("s_xt")
        s_xe = sem("s_xe")
        s_gu = sem("s_gu")
        s_th = sem("s_th")
        s_ha = sem("s_ha")
        s_h = sem("s_h")
        s_tr = sem("s_tr")
        s_ht = sem("s_ht")
        s_y = sem("s_y")
        s_ye = sem("s_ye")
        s_ys = [sem("s_ys0"), sem("s_ys1")]
        s_rv = sem("s_rv")
        s_re = sem("s_re")
        s_wk = sem("s_wk")
        s_ex = sem("s_ex")
        s_cu = sem("s_cu")
        s_l1 = sem("s_l1")
        s_gy = [sem(f"s_gy{n}") for n in range(4)]
        s_zz = sem("s_zz")
        s_at = sem("s_at")
        s_e = sem("s_e")
        s_a1 = sem("s_a1")
        s_v1 = sem("s_v1")
        s_q1 = sem("s_q1")
        s_ln = sem("s_ln")
        s_xq = sem("s_xq")
        s_xca = sem("s_xca")
        s_xcv = sem("s_xcv")
        s_w1 = sem("s_w1")
        s_qt = sem("s_qt")
        s_qe = sem("s_qe")
        s_f = sem("s_f")
        s_fa = sem("s_fa")
        s_wb = sem("s_wb")
        s_zp = sem("s_zp")
        s_za = sem("s_za")
        s_sd2 = sem("s_sd2")
        s_sp = sem("s_sp")
        s_sv = sem("s_sv")
        s_sh = sem("s_sh")
        s_fz = sem("s_fz")
        s_o = [sem("s_o0"), sem("s_o1")]
        block = ctx.enter_context(nc.Block())

        N_CONST = 10
        N_SMALL = 9

        def stepper(s):
            count = [0]

            def step(eng, ins):
                ins.then_inc(s, 1)
                count[0] += 1
                eng.wait_ge(s, count[0])
            return step

        ROUND_TILES = 4
        PIECES = [(0, 1), (2, None), (3, 4), (5, None)]
        DONE = [0, 2, 3, 5]
        TAIL = 1 + ROUND_TILES * (ROUNDS - 1)
        PEEL = 2

        @block.sync
        def _(sp):
            for n in range(4):
                sp.dma_start(x_in[:, 4 * n:4 * n + 4, :], x_v[:, 4 * n:4 * n + 4, :]).then_inc(s_x[n], 16)
            sp.wait_ge(s_k, 1)
            sp.dma_start(slots_x.rearrange("(i p) c -> p i c", p=P),
                         zero.unsqueeze(1).to_broadcast([P, LOADS, C])).then_inc(s_zf, 16)
            for e in range(NE):
                sp.dma_start(wg[:, e], w_g[e].rearrange("(k p) f -> p k f", p=P)).then_inc(s_we[e], 16)
                sp.dma_start(wu[:, e], w_u[e].rearrange("(k p) f -> p k f", p=P)).then_inc(s_we[e], 16)
                sp.dma_start(wd[:, e], w_d[e].rearrange("(k p) c -> p k c", p=P)).then_inc(s_we[e], 16)
                if e:
                    sp.wait_ge(s_we[e - 1], 48)
                    sp.sem_inc(s_wt, 1)
            sp.wait_ge(s_we[NE - 1], 48)
            sp.sem_inc(s_wt, 1)
            for n in range(RING):
                sp.dma_start(ring[:, n, :], blocks[n]).then_inc(s_bk[n], 16)
            full = NBLK // RING

            def refill(n, slot):
                sp.wait_ge(s_ba, n - RING + 2)
                sp.dma_start(ring[:, slot, :], blocks[ds(n, 1)].rearrange("a p w -> p (a w)"))\
                    .then_inc(s_bk[slot], 16)

            with sp.Fori(1, full) as i:
                for n in range(RING):
                    refill(RING * i + n, n)
            for n in range(full * RING, NBLK):
                refill(n, n % RING)
            sp.wait_ge(s_wk, UNIT * 2 * ROUNDS)
            sp.dma_start(wout_sb, w_out.rearrange("(k p) c -> p k c", p=P)).then_inc(s_l1, 16)
            sp.dma_start(x1, x_v).then_inc(s_l1, 16)
            sp.dma_start(wt_sb, w_t.rearrange("(k p) c -> p k c", p=P)).then_inc(s_l1, 16)
            sp.dma_start(rr_sb, rram.rearrange("(k p) c -> p k c", p=P)).then_inc(s_l1, 16)
            sp.wait_ge(s_cv, 1)
            many = sp.value_load(pairs_i[0:1, 0:1], min_val=0, max_val=NBLK)
            with sp.If(many > SLOTS):
                sp.wait_ge(s_zp, SLOTS + 1)
                sp.wait_ge(s_ht, 2 * MT)
                with sp.Fori(0, NBLK) as n:
                    sp.wait_ge(s_sp, n + 1)
                    sp.dma_start(spare, blocks[ds(n, 1)].rearrange("a p w -> p (a w)")).then_inc(s_sd2, 16)
            for jj in range(NROW // 2):
                sp.wait_ge(s_fz, 3 * jj + 4)
                sp.dma_start(out_v[:, jj:NT:NROW // 2, :], res[:, jj % 2]).then_inc(s_o[jj % 2], 16)
            for n in range(2):
                sp.wait_ge(s_o[n], 16 * (NROW // 4))

        @block.gpsimd
        def _(g):
            step = stepper(s_k)
            step(g, g.memset(zero, 0.0))
            step(g, g.memset(ones[:, :], 1.0))
            step(g, g.memset(ident[:, :], 0.0))
            step(g, g.affine_select(out=ident[:, :], in_=ident[:, :], compare_op=ALU.not_equal, fill=1.0,
                                    base=0, pattern=[[-1, P]], channel_multiplier=1))
            step(g, g.affine_select(out=before[:, :], in_=ones[:, :], compare_op=ALU.is_gt, fill=0.0,
                                    base=0, pattern=[[1, P]], channel_multiplier=-1))
            step(g, g.affine_select(out=after, in_=ones[:, :], compare_op=ALU.is_gt, fill=0.0,
                                    base=0, pattern=[[-1, P]], channel_multiplier=1))
            step(g, g.iota(iota, pattern=[[1, P]], base=0, channel_multiplier=0,
                           allow_small_or_imprecise_dtypes=True))
            step(g, g.iota(iota_r, pattern=[[-1, P]], base=P, channel_multiplier=0,
                           allow_small_or_imprecise_dtypes=True))
            step(g, g.iota(starts[:, :], pattern=[[P, NT]], base=0, channel_multiplier=0,
                           allow_small_or_imprecise_dtypes=True))
            step(g, g.iota(tiles[:, :], pattern=[[1, LOADS]], base=0, channel_multiplier=0,
                           allow_small_or_imprecise_dtypes=True))
            g.wait_ge(s_pos, 1)
            g.wait_ge(s_xn, NT)
            g.wait_ge(s_zf, 16)
            for i in range(NT):
                g.indirect_dma_start(out=slots_x, out_offset=bass.IndirectOffsetOnAxis(ap=pos_i[:, i:i + 1], axis=0),
                                     in_=xn[:, i, :], in_offset=None).then_inc(s_sc, 16)
            g.wait_ge(s_sc, 16 * NT)
            g.wait_ge(s_tp, NT // 2)
            g.memset(acc[:, :], 0.0).then_inc(s_ba, 1)
            g.wait_ge(s_cv, 1)

            def add_block(n, place, turn):
                slot = g.value_load(slot_i[0:1, ds(n, 1)], min_val=0, max_val=SLOTS)
                g.wait_ge(s_bk[place], 16 * turn)
                g.wait_ge(s_ba, n + 1)
                a = accs[:, ds(slot, 1), :].rearrange("p a w -> p (a w)")
                g.tensor_tensor(a, a, ring[:, place, :], ALU.add).then_inc(s_ba, 1)

            with g.Fori(0, NBLK // RING) as i:
                for n in range(RING):
                    add_block(RING * i + n, n, i + 1)
            for n in range(NBLK // RING * RING, NBLK):
                add_block(n, n % RING, n // RING + 1)
            for n in range(2):
                g.wait_ge(s_ys[n], 16 * ((MT + 1 - n) // 2 + 1))
            for i in range(NT):
                g.indirect_dma_start(out=yg[:, i, :], out_offset=None, in_=slots_y,
                                     in_offset=bass.IndirectOffsetOnAxis(ap=pos_i[:, i:i + 1], axis=0))\
                    .then_inc(s_gy[i // 4], 16)
            g.memset(xc[:, :, :, 0:KS], 0.0).then_inc(s_zz, 1)
            g.memset(z, 0.0).then_inc(s_zz, 1)

        @block.scalar
        def _(a):
            a.dma_start(wrvk_sb[:, :, :], w_rvk.rearrange("(k p) c -> p k c", p=P)).then_inc(s_c, 16)
            a.dma_start(wr_sb[:, :, :], w_r.rearrange("(k p) e -> p k e", p=P)).then_inc(s_c, 16)
            a.dma_start(br_sb[:, :], b_r.partition_broadcast(P)).then_inc(s_c, 16)
            a.dma_start(dec[:, :], decay).then_inc(s_c, 16)
            a.dma_start(uv[:, :], first).then_inc(s_c, 16)
            a.dma_start(rows_i[:, :], rows.partition_broadcast(P)).then_inc(s_c, 16)
            a.dma_start(cols_i[:, :], cols.partition_broadcast(P)).then_inc(s_c, 16)
            a.dma_start(rc_i[:, 0:1], rows.unsqueeze(1)).then_inc(s_c, 16)
            a.dma_start(rc_i[:, 1:2], cols.unsqueeze(1)).then_inc(s_c, 16)
            a.wait_ge(s_ve, 1)
            a.activation(ve[:, :], ve[:, :], ACT.Sqrt).then_inc(s_sd, 1)
            for n in range(0, NT // 2, 2):
                a.wait_ge(s_tp, n + 1)
                a.activation(tr[:, :, col_of(2 * n):col_of(2 * n) + 2 * P].rearrange("p k (t n) -> p k t n", t=2),
                             four[n % 4][:, :].rearrange("p (t k n) -> p k t n", t=2, k=KC), ACT.Copy)\
                    .then_inc(s_ta, 1)
            a.wait_ge(s_c, 16 * N_SMALL)
            a.activation(wv[:, :], dec[:, :], ACT.Exp).then_inc(s_cu, 1)

            def piece(j, p, src):
                c, kind = p // 3, p % 3
                a.wait_ge(s_rv, RP * j + p + 1)
                dst = kvr[:, c, kind, :]
                if kind == 2:
                    a.activation(dst, src[:, :], ACT.Tanh, scale=0.5).then_inc(s_re, 1)
                else:
                    a.activation(dst, src[:, :], ACT.Copy).then_inc(s_re, 1)

            def exps(n, c):
                for m, (buf, bias, at_) in enumerate([(b2, None, 4), (b1, uv, 5), (b3, wv, 6),
                                                     (opq[:, 2, 1:QT + 1], None, 7)]):
                    a.wait_ge(s_wk, UNIT * n + at_)
                    if bias is None:
                        a.activation(buf, buf, ACT.Exp).then_inc(s_ex, 1)
                    else:
                        a.activation(buf, buf, ACT.Exp, bias=bias[:, c:c + 1]).then_inc(s_ex, 1)

            def load_slot_tile(s):
                a.dma_start(xs[:, :], slots_x[ds(s * P, P), :]).then_inc(s_xs, 16)

            def slot_tile_out(s, par):
                a.wait_ge(s_xt, s + 1)
                a.activation(xs_t[:, par, :, :], pr[:, 0:KC * P].rearrange("p (k n) -> p k n", k=KC), ACT.Copy)\
                    .then_inc(s_xe, 1)
                load_slot_tile(s + 1)

            def half_t(s, f):
                a.wait_ge(s_tr, 2 * s + f + 1)
                a.activation(h_t[:, 4 * f:4 * f + 4, :], pt[f][:, :].rearrange("p (k n) -> p k n", k=4), ACT.Copy)\
                    .then_inc(s_ht, 1)

            def tanh(s, f):
                a.wait_ge(s_gu, 2 * s + f + 1)
                a.activation(th[:, f, :], pg[f][:, :], ACT.Tanh, scale=0.5).then_inc(s_th, 1)

            def y_out(s, par, reuse):
                a.wait_ge(s_y, s + 1)
                a.wait_ge(s_ys[par], reuse + 16)
                a.activation(y_sb[:, par, :], py[:, 0:C], ACT.Copy).then_inc(s_ye, 1)
                a.wait_ge(s_ye, s + 1)
                a.dma_start(slots_y[ds(s * P, P), :], y_sb[:, par, :]).then_inc(s_ys[par], 16)

            def tile(s, par, slot2=None, slot3=None, unit=None, first_tile=False, stored=None):
                tanh(s, 0)
                if not first_tile:
                    half_t(s - 1, 1)
                slot_tile_out(s + 1, 1 - par)
                tanh(s, 1)
                if slot2:
                    slot2()
                if not first_tile:
                    y_out(s - 1, 1 - par, stored)
                half_t(s, 0)
                if unit:
                    unit()
                if slot3:
                    slot3()

            for n in range(2):
                a.sem_inc(s_ys[n], 16)
            for p in range(RP):
                if p == 1:
                    a.wait_ge(s_sub, 1)
                    a.activation(ex, lg, ACT.Exp).then_inc(s_el, 1)
                piece(0, p, six[p])
            exps(0, 0)
            a.wait_ge(s_sc, 16 * NT)
            load_slot_tile(0)
            slot_tile_out(0, 0)
            tile(0, 0, first_tile=True)
            with a.Fori(0, ROUNDS - 1) as it:
                for jj in range(ROUND_TILES):
                    s = it * ROUND_TILES + (1 + jj)
                    par = (1 + jj) % 2
                    n_before = it * 2 + (jj // 2)
                    slots = []
                    for p in PIECES[jj]:
                        if p is None:
                            slots.append(None)
                            continue

                        def place(p=p, it=it):
                            if p % 3 == 0:
                                a.wait_ge(s_wk, (it * 2 + (p // 3 + 1)) * UNIT)
                            piece(it + 1, p, pr)
                        slots.append(place)
                    unit = None
                    if jj == 0:
                        def unit(it=it):
                            exps(it * 2 + 1, 1)
                    if jj == 2:
                        def unit(it=it):
                            exps(it * 2 + 2, 0)
                    tile(s, par, slots[0], slots[1], unit, stored=n_before * 16)
            for s in range(TAIL, TAIL + PEEL):
                tile(s, s % 2, unit=(lambda: exps(2 * ROUNDS - 1, 1)) if s == TAIL else None,
                     stored=((s - 1) // 2) * 16)
            with a.Fori(0, (MT - TAIL - PEEL) // 2) as it:
                for jj in range(2):
                    s = it * 2 + (TAIL + PEEL + jj)
                    tile(s, (TAIL + PEEL + jj) % 2, stored=(it + (TAIL + PEEL + jj - 1) // 2) * 16)
            half_t(MT - 1, 1)
            y_out(MT - 1, (MT - 1) % 2, ((MT - 1) // 2) * 16)
            for m in range(4):
                a.wait_ge(s_v1, m + 1)
                a.activation(ve[:, 4 * m:4 * m + 4], ve[:, 4 * m:4 * m + 4], ACT.Sqrt).then_inc(s_q1, 1)
                for i in range(4 * m, 4 * m + 4):
                    b, r = i // 8, 2 * (i % 8)
                    a.wait_ge(s_ln, i + 1)
                    if i == 0:
                        a.wait_ge(s_zz, 1)
                    a.activation(xc[64:128, b, r, KS - 2:KS - 2 + C], xln[0:64, i % 4, :], ACT.Copy).then_inc(s_xca, 1)
                    a.activation(xc[0:64, b, r + 1, KS - 1:KS - 1 + C], xln[64:128, i % 4, :], ACT.Copy)\
                        .then_inc(s_xca, 1)
                    a.wait_ge(s_qt, i + 1)
                    a.activation(tr[:, :, col_of(i):col_of(i) + P],
                                 pt[i % 2][:, 0:KC * P].rearrange("p (k n) -> p k n", k=KC), ACT.Copy).then_inc(s_qe, 1)
            with a.Fori(0, SLOTS // 2) as it:
                for n in range(2):
                    s = it * 2 + n
                    a.wait_ge(s_ba, NBLK + 1)
                    a.wait_ge(s_zp, it * 2 + 1)
                    a.activation(wbuf[:, n, :], accs[:, ds(s, 1), :].rearrange("p a w -> p (a w)"), ACT.Copy)\
                        .then_inc(s_wb, 1)
            a.wait_ge(s_za, SLOTS + 1)
            a.wait_ge(s_fz, 1)
            for jj in range(NROW // 2):
                if jj >= 2:
                    a.wait_ge(s_fz, 3 * (jj - 1) + 1)
                a.activation(shifted[0:64, jj % 2], z[64:128, 2 * jj, :, TAPS:TAPS + C], ACT.Copy).then_inc(s_sh, 1)
                a.activation(shifted[64:128, jj % 2], z[0:64, 2 * jj + 1, :, 0:C], ACT.Copy).then_inc(s_sh, 1)

        @block.tensor
        def _(t):
            t.wait_ge(s_k, N_CONST)
            for n in range(NT // 2):
                t.wait_ge(s_xn, 2 * n + 2)
                if n >= 4:
                    if n % 2 == 0:
                        t.wait_ge(s_ta, (n - 4) // 2 + 1)
                    else:
                        t.wait_ge(s_tv, (n - 5) // 2 + 1)
                for tt in range(2):
                    for k in range(KC):
                        q = (tt * KC + k) * P
                        mm = t.transpose(four[n % 4][:, q:q + P], xn[:, 2 * n + tt, k * P:(k + 1) * P], ident[:, :])
                mm.then_inc(s_tp, 1)
            t.wait_ge(s_ta, NT // 4)
            t.wait_ge(s_tv, NT // 4)
            t.wait_ge(s_c, 16 * N_SMALL)
            for i in range(NT):
                for k in range(KC):
                    mm = t.matmul(pr[:, NE * i:NE * i + NE], tr[:, k, col_of(i):col_of(i) + P], wr_sb[:, k, :],
                                  start=(k == 0), stop=(k == KC - 1))
            mm.then_inc(s_lg, 1)

            def piece(j, p, dst):
                c, kind = p // 3, p % 3
                w0 = (2 - kind) * C + c * P
                for k in range(KC):
                    mm = t.matmul(dst[:, :], wrvk_sb[:, k, w0:w0 + P], tr[:, k, ds(j * QT, QT)],
                                  start=(k == 0), stop=(k == KC - 1))
                mm.then_inc(s_rv, 1)

            for p in range(RP):
                piece(0, p, six[p])
            t.wait_ge(s_oh, 1)
            t.matmul(pr[:, 64:128], before[:, :], oh.rearrange("p i e -> p (i e)"), start=True, stop=True)
            t.matmul(pr[:, 128:192], ones[:, :], oh.rearrange("p i e -> p (i e)"), start=True, stop=True)\
                .then_inc(s_cn, 1)
            t.wait_ge(s_fb, 1)
            t.wait_ge(s_pos, 1)
            t.matmul(pr[:, 0:P], first_b, before[:, :], start=True, stop=True).then_inc(s_gp, 1)
            t.wait_ge(s_gd, 1)
            t.matmul(pr[:, 0:P], ones[:, :], gid_d, start=True, stop=True)
            t.matmul(pr[:, 128:128 + SLOTS], row_b, sel, start=True, stop=True)
            t.matmul(pr[:, 144:144 + SLOTS], col_b, sel, start=True, stop=True)
            t.matmul(pr[:, 160:161], first_b, ones[:, 0:1], start=True, stop=True).then_inc(s_gt, 1)

            def gate_up(s, par, f, e):
                for dst, w in ((pg[f], wg), (pu[f], wu)):
                    for k in range(KC):
                        mm = t.matmul(dst[:, :], xs_t[:, par, k, :],
                                      w[:, ds(e, 1), k, 512 * f:512 * f + 512].rearrange("p a f -> p (a f)"),
                                      start=(k == 0), stop=(k == KC - 1))
                mm.then_inc(s_gu, 1)

            def turn_h(s, f):
                t.wait_ge(s_h, 2 * s + f + 1)
                for k in range(4):
                    q = 4 * f + k
                    mm = t.transpose(pt[f][:, k * P:(k + 1) * P], h[:, q * P:(q + 1) * P], ident[:, :])
                mm.then_inc(s_tr, 1)

            def turn_slots(s):
                t.wait_ge(s_xs, 16 * (s + 1))
                for k in range(KC):
                    mm = t.transpose(pr[:, k * P:(k + 1) * P], xs[:, k * P:(k + 1) * P], ident[:, :])
                mm.then_inc(s_xt, 1)

            def down(s):
                e = t.value_load(eid_i[0:1, ds(s, 1)], min_val=0, max_val=NE - 1)
                t.wait_ge(s_ht, 2 * s + 2)
                t.wait_ge(s_ye, s)
                for k in range(KF):
                    mm = t.matmul(py[:, 0:C], h_t[:, k, :], wd[:, ds(e, 1), k, :].rearrange("p a c -> p (a c)"),
                                  start=(k == 0), stop=(k == KF - 1))
                mm.then_inc(s_y, 1)

            def tile(s, par, pieces_before, slot2=None, slot3=None, first_tile=False):
                e = t.value_load(eid_i[0:1, ds(s, 1)], min_val=0, max_val=NE - 1)
                t.wait_ge(s_wt, e + 1)
                t.wait_ge(s_xe, s + 1)
                if not first_tile:
                    t.wait_ge(s_h, 2 * s - 1)
                gate_up(s, par, 0, e)
                if not first_tile:
                    turn_h(s - 1, 1)
                t.wait_ge(s_re, pieces_before)
                turn_slots(s + 1)
                if not first_tile:
                    t.wait_ge(s_h, 2 * s)
                gate_up(s, par, 1, e)
                if slot2:
                    t.wait_ge(s_xe, s + 2)
                    slot2()
                if not first_tile:
                    down(s - 1)
                turn_h(s, 0)
                if slot3:
                    slot3()

            t.wait_ge(s_pos, 1)
            t.wait_ge(s_re, RP)
            t.wait_ge(s_cv, 1)
            turn_slots(0)
            t.wait_ge(s_xe, 1)
            tile(0, 0, RP, first_tile=True)
            with t.Fori(0, ROUNDS - 1) as it:
                for jj in range(ROUND_TILES):
                    slots = []
                    for n, p in enumerate(PIECES[jj]):
                        if p is None:
                            slots.append(None)
                            continue

                        def place(p=p, it=it, n=n):
                            if n:
                                t.wait_ge(s_re, it * RP + (RP + p))
                            piece(it + 1, p, pr)
                        slots.append(place)
                    tile(it * ROUND_TILES + (1 + jj), (1 + jj) % 2, it * RP + (RP + DONE[jj]), slots[0], slots[1])
            for s in range(TAIL, TAIL + PEEL):
                tile(s, s % 2, RP * ROUNDS)
            with t.Fori(0, (MT - TAIL - PEEL) // 2) as it:
                for jj in range(2):
                    tile(it * 2 + (TAIL + PEEL + jj), (TAIL + PEEL + jj) % 2, RP * ROUNDS)
            turn_h(MT - 1, 1)
            down(MT - 1)
            t.wait_ge(s_l1, 64)
            t.wait_ge(s_wk, UNIT * 2 * ROUNDS)

            def attend(i):
                if i >= 2:
                    t.wait_ge(s_a1, i - 1)
                for k in range(KC):
                    mm = t.matmul(pg[i % 2][:, 0:C], tr[:, k, col_of(i):col_of(i) + P], wout_sb[:, k, :],
                                  start=(k == 0), stop=(k == KC - 1))
                mm.then_inc(s_at, 1)

            def dense(i):
                t.wait_ge(s_qe, i + 1)
                if i >= 4:
                    t.wait_ge(s_fa, i - 3)
                for k in range(KC):
                    mm = t.matmul(dense_bank[i % 4][:, 0:C], tr[:, k, col_of(i):col_of(i) + P], wt_sb[:, k, :],
                                  start=(k == 0), stop=(k == KC - 1))
                mm.then_inc(s_f, 1)

            for i in range(4):
                attend(i)
            t.wait_ge(s_w1, 1)
            for i in range(NT):
                t.wait_ge(s_xq, i + 1)
                if i >= 2:
                    t.wait_ge(s_qe, i - 1)
                for k in range(KC):
                    mm = t.transpose(pt[i % 2][:, k * P:(k + 1) * P], xq[:, i % 4, k * P:(k + 1) * P], ident[:, :])
                mm.then_inc(s_qt, 1)
                if i:
                    dense(i - 1)
                if i + 4 < NT:
                    attend(i + 4)
            dense(NT - 1)
            t.wait_ge(s_xca, 2 * NT)
            t.wait_ge(s_xcv, 2 * NT)
            t.wait_ge(s_fa, NT)
            t.wait_ge(s_a1, NT)
            pz = [(pg[0], pg[1]), (pu[0], pu[1])]

            def conv(w, c, banks):
                for b in range(BATCH):
                    for j in range(TAPS // 2):
                        mm = t.matmul(banks[b][:, 0:SPAN], w[:, j * P:(j + 1) * P],
                                      xc[:, b, ds(c, 1), 2 * j:2 * j + SPAN].rearrange("p a u -> p (a u)"),
                                      start=(j == 0), stop=(j == TAPS // 2 - 1))
                return mm

            t.sem_inc(s_zp, 1)
            with t.Fori(0, SLOTS // 2) as it:
                for n in range(2):
                    s = it * 2 + n
                    c = t.value_load(scol_i[0:1, ds(s, 1)], min_val=0, max_val=NROW - 1)
                    t.wait_ge(s_wb, s + 1)
                    t.wait_ge(s_za, it * 2 + 1)
                    conv(wbuf[:, n, :], c, pz[n]).then_inc(s_zp, 1)
            many = t.value_load(pairs_i[0:1, 0:1], min_val=0, max_val=NBLK)
            with t.If(many > SLOTS):
                t.sem_inc(s_sp, 1)
                with t.Fori(0, NBLK) as n:
                    c = t.value_load(cols_i[0:1, ds(n, 1)], min_val=0, max_val=NROW - 1)
                    t.wait_ge(s_sd2, n * 16 + 16)
                    t.wait_ge(s_sv, n + 1)
                    t.wait_ge(s_za, SLOTS + 1)
                    conv(spare, c, pz[0]).then_inc(s_sp, 1)

        @block.vector
        def _(v):
            step = stepper(s_p)
            v.wait_ge(s_k, N_CONST)
            for n in range(4):
                v.wait_ge(s_x[n], 16)
                for i in range(4 * n, 4 * n + 4):
                    ins = v.bn_stats(stats[:, i, :], x_in[:, i, :])
            step(v, ins)
            for i in range(NT):
                ins = v.bn_aggr(mv[:, i, :], stats[:, i, :])
            step(v, ins)
            v.tensor_scalar(ve[:, :], mv[:, :, 1], EPS, None, ALU.add).then_inc(s_ve, 1)
            v.wait_ge(s_sd, 1)
            step(v, v.reciprocal(rstd[:, :], ve[:, :]))
            for i in range(NT):
                v.tensor_scalar(xn[:, i, :], x_in[:, i, :], mv[:, i, 0:1], rstd[:, i:i + 1], ALU.subtract, ALU.mult)\
                    .then_inc(s_xn, 1)
            for n in range(1, NT // 2, 2):
                v.wait_ge(s_tp, n + 1)
                v.tensor_copy(tr[:, :, col_of(2 * n):col_of(2 * n) + 2 * P].rearrange("p k (t n) -> p k t n", t=2),
                              four[n % 4][:, :].rearrange("p (t k n) -> p k t n", t=2, k=KC)).then_inc(s_tv, 1)
            v.wait_ge(s_c, 16 * N_SMALL)
            v.wait_ge(s_lg, 1)
            step(v, v.tensor_tensor(lg, pr[:, 0:64].rearrange("p (i e) -> p i e", e=NE),
                                    br_sb[:, :].unsqueeze(1).to_broadcast([P, NT, NE]), ALU.add))
            step(v, v.tensor_reduce(mx, lg, AX.X, ALU.max))
            v.tensor_tensor(lg, lg, mx.unsqueeze(2).to_broadcast([P, NT, NE]), ALU.subtract).then_inc(s_sub, 1)
            v.wait_ge(s_sub, 1)
            step(v, v.tensor_scalar(eq, lg, 0.0, None, ALU.is_ge))
            step(v, v.tensor_copy(oh[:, :, 0], eq[:, :, 0]))
            step(v, v.tensor_copy(seen, eq[:, :, 0]))
            for e in range(1, NE):
                ins = v.tensor_tensor(oh[:, :, e], eq[:, :, e], seen, ALU.is_gt)
                if e < NE - 1:
                    step(v, ins)
                    step(v, v.tensor_tensor(seen, seen, eq[:, :, e], ALU.max))
            ins.then_inc(s_oh, 1)
            step(v, v.scalar_tensor_tensor(out=key, in0=rows_i[:, :], scalar=float(NROW), in1=cols_i[:, :],
                                           op0=ALU.mult, op1=ALU.add))
            step(v, v.scalar_tensor_tensor(out=keyc, in0=rc_i[:, 0:1], scalar=float(NROW), in1=rc_i[:, 1:2],
                                           op0=ALU.mult, op1=ALU.add))
            step(v, v.tensor_copy(rowf, rc_i[:, 0:1]))
            step(v, v.tensor_copy(colf, rc_i[:, 1:2]))
            step(v, v.tensor_scalar(same, key, keyc, None, ALU.is_equal))
            step(v, v.tensor_tensor(tmp, same, after, ALU.mult))
            step(v, v.tensor_reduce(seenc, tmp, AX.X, ALU.add))
            step(v, v.tensor_scalar(firstc, seenc, 0.0, None, ALU.is_equal))
            v.tensor_scalar(first_b, ones[:, :], firstc, None, ALU.mult).then_inc(s_fb, 1)
            step(v, v.tensor_tensor(tmp, same, iota_r, ALU.mult))
            step(v, v.tensor_reduce(fidx, tmp, AX.X, ALU.max))
            step(v, v.tensor_scalar(fidx, fidx, -1.0, float(P), ALU.mult, ALU.add))
            step(v, v.tensor_scalar(same, iota, fidx, None, ALU.is_equal))
            v.wait_ge(s_el, 1)
            step(v, v.tensor_reduce(sums, ex, AX.X, ALU.add))
            step(v, v.reciprocal(top_w[:, :], sums))
            v.wait_ge(s_cn, 1)
            total = pr[:, 128:192].rearrange("p (i e) -> p e i", e=NE)
            for e in range(NE):
                ins = v.tensor_tensor_scan(incl[:, e, :], ones[:, 0:NT], total[:, e, :], 0.0, ALU.mult, ALU.add)
            step(v, ins)
            step(v, v.tensor_tensor(cmp, incl[:, :, NT - 1:NT].to_broadcast([P, NE, NT]),
                                    starts[:, :].unsqueeze(1).to_broadcast([P, NE, NT]), ALU.is_gt))
            step(v, v.tensor_reduce(t_e, cmp, AX.X, ALU.add))
            step(v, v.tensor_tensor_scan(t_end, ones[:, 0:NE], t_e, 0.0, ALU.mult, ALU.add))
            step(v, v.tensor_tensor(t_beg, t_end, t_e, ALU.subtract))
            step(v, v.tensor_tensor(ps, incl.rearrange("p e i -> p i e"), pr[:, 64:128].rearrange(
                "p (i e) -> p i e", e=NE), ALU.add))
            step(v, v.tensor_tensor(ps, ps, pr[:, 128:192].rearrange("p (i e) -> p i e", e=NE), ALU.subtract))
            step(v, v.tensor_scalar(t_beg, t_beg, float(P), None, ALU.mult))
            step(v, v.tensor_tensor(ps, ps, t_beg.unsqueeze(1).to_broadcast([P, NT, NE]), ALU.add))
            step(v, v.tensor_tensor(ps, ps, oh, ALU.mult))
            step(v, v.tensor_reduce(pos, ps, AX.X, ALU.add))
            step(v, v.tensor_copy(pos_i[:, :], pos))
            step(v, v.tensor_tensor(ecmp, tiles[:, :].unsqueeze(2).to_broadcast([P, LOADS, 3]),
                                    t_end[:, 0:3].unsqueeze(1).to_broadcast([P, LOADS, 3]), ALU.is_ge))
            step(v, v.tensor_reduce(eid, ecmp, AX.X, ALU.add))
            v.tensor_copy(eid_i[:, :], eid).then_inc(s_pos, 1)
            v.wait_ge(s_gp, 1)
            step(v, v.tensor_tensor(tmp, same, pr[:, 0:P], ALU.mult))
            step(v, v.tensor_reduce(gid, tmp, AX.X, ALU.add))
            step(v, v.tensor_scalar(gid_d, ident[:, :], gid, None, ALU.mult))
            step(v, v.tensor_scalar(row_b, ones[:, :], rowf, None, ALU.mult))
            step(v, v.tensor_scalar(col_b, ones[:, :], colf, None, ALU.mult))
            v.tensor_scalar(sel, iota[:, 0:SLOTS], gid, firstc, ALU.is_equal, ALU.mult).then_inc(s_gd, 1)
            v.wait_ge(s_gt, 1)
            step(v, v.tensor_scalar(slot_i[:, :], pr[:, 0:P], float(SLOTS), None, ALU.min))
            step(v, v.tensor_scalar(spill[:, :], pr[:, 0:P], float(SLOTS), None, ALU.is_ge))
            step(v, v.tensor_copy(srow_i[:, :], pr[:, 128:128 + SLOTS]))
            step(v, v.tensor_copy(scol_i[:, :], pr[:, 144:144 + SLOTS]))
            v.tensor_copy(pairs_i[:, :], pr[:, 160:161]).then_inc(s_cv, 1)
            step(v, v.memset(carry[:, :, :, 0:1], -1e38))
            step(v, v.memset(carry[:, :, :, 1:3], 0.0))
            v.wait_ge(s_cu, 1)
            step(v, v.tensor_scalar(wv[:, :], wv[:, :], -1.0, None, ALU.mult))

            def wkv(n, j, c, part_):
                kk, vv, tt = kvr[:, c, 0, :], kvr[:, c, 1, :], kvr[:, c, 2, :]
                o_old, o_new = opq[:, 0, 0:QT], opq[:, 0, 1:QT + 1]
                p_old, p_new = opq[:, 1, 0:QT], opq[:, 1, 1:QT + 1]
                q_old, q_new = opq[:, 2, 0:QT], opq[:, 2, 1:QT + 1]
                w_b = wv[:, c:c + 1].to_broadcast([P, QT])
                tt_ = v.tensor_tensor
                stt = v.scalar_tensor_tensor
                pieces = RP * j + 3 * c
                steps = [
                    lambda: v.tensor_copy(opq[:, :, 0:1], carry[:, c, ds(j, 1), :].rearrange("p a q -> p q a")),
                    lambda: v.tensor_tensor_scan(o_new, w_b, kk, opq[:, 0, 0:1], ALU.add, ALU.max),
                    lambda: stt(out=b1, in0=kk, scalar=uv[:, c:c + 1], in1=o_old, op0=ALU.add, op1=ALU.max),
                    lambda: tt_(b2, o_old, b1, ALU.subtract),
                    lambda: tt_(b1, kk, b1, ALU.subtract),
                    lambda: tt_(b3, o_old, o_new, ALU.subtract),
                    lambda: tt_(q_new, kk, o_new, ALU.subtract),
                    lambda: tt_(p_new, q_new, vv, ALU.mult),
                    lambda: v.tensor_tensor_scan(p_new, b3, p_new, opq[:, 1, 0:1], ALU.mult, ALU.add),
                    lambda: v.tensor_tensor_scan(q_new, b3, q_new, opq[:, 2, 0:1], ALU.mult, ALU.add),
                    lambda: tt_(b3, b2, p_old, ALU.mult),
                    lambda: tt_(kk, b1, vv, ALU.mult),
                    lambda: tt_(b3, b3, kk, ALU.add),
                    lambda: tt_(b2, b2, q_old, ALU.mult),
                    lambda: tt_(b2, b2, b1, ALU.add),
                    lambda: v.tensor_copy(carry[:, c, ds(j + 2, 1), :].rearrange("p a q -> p q a"),
                                          opq[:, :, QT:QT + 1]),
                    lambda: v.reciprocal(b2, b2),
                    lambda: stt(out=b3, in0=tt, scalar=1.0, in1=b3, op0=ALU.add, op1=ALU.mult),
                    lambda: stt(out=tr[:, c, ds(j * QT, QT)], in0=b3, scalar=0.5, in1=b2, op0=ALU.mult, op1=ALU.mult),
                ]
                assert len(steps) == UNIT
                waits = {1: [(s_re, pieces + 1)],
                         7: [(s_re, pieces + 2), (s_ex, 4 * n + 4)],
                         17: [(s_re, pieces + 3)],
                         18: [(s_rv, RP * j + RP)]}
                for q in range(*part_):
                    for s_, val in waits.get(q, []):
                        v.wait_ge(s_, val)
                    v.wait_ge(s_wk, UNIT * n + q)
                    steps[q]().then_inc(s_wk, 1)

            def act_half(s, f):
                v.wait_ge(s_th, 2 * s + f + 1)
                v.scalar_tensor_tensor(out=th[:, f, :], in0=th[:, f, :], scalar=1.0, in1=pu[f][:, :],
                                       op0=ALU.add, op1=ALU.mult).then_inc(s_ha, 1)
                v.wait_ge(s_ha, 2 * s + f + 1)
                v.scalar_tensor_tensor(out=h[:, 512 * f:512 * f + 512], in0=pg[f][:, :], scalar=0.5,
                                       in1=th[:, f, :], op0=ALU.mult, op1=ALU.mult).then_inc(s_h, 1)

            def tile(s, unit=None, part_a=None, part_b=None):
                act_half(s, 0)
                if unit:
                    wkv(*unit, part_a)
                act_half(s, 1)
                if unit:
                    wkv(*unit, part_b)

            PARTS = [((0, 3), (3, 7)), ((7, 13), (13, UNIT))]
            v.wait_ge(s_p, 1)
            wkv(0, 0, 0, (0, UNIT))
            tile(0)
            with v.Fori(0, ROUNDS - 1) as it:
                for jj in range(ROUND_TILES):
                    unit = (it * 2 + 1, it, 1) if jj < 2 else (it * 2 + 2, it + 1, 0)
                    tile(it * ROUND_TILES + (1 + jj), unit, *PARTS[jj % 2])
            for s in range(TAIL, TAIL + PEEL):
                tile(s, (2 * ROUNDS - 1, ROUNDS - 1, 1), *PARTS[s - TAIL])
            with v.Fori(0, (MT - TAIL - PEEL) // 2) as it:
                for jj in range(2):
                    tile(it * 2 + (TAIL + PEEL + jj))
            step = stepper(s_e)
            v.wait_ge(s_l1, 64)
            pos_w, neg_w = th[:, 0, :].rearrange("p (k c) -> p k c", k=KC), th[:, 1, :].rearrange("p (k c) -> p k c", k=KC)
            step(v, v.tensor_scalar(pos_w, wt_sb, TH_W, SC_W, ALU.is_gt, ALU.mult))
            step(v, v.tensor_scalar(neg_w, wt_sb, -TH_W, -SC_W, ALU.is_lt, ALU.mult))
            step(v, v.tensor_tensor(pos_w, pos_w, neg_w, ALU.add))
            step(v, v.tensor_tensor(pos_w, pos_w, rr_sb, ALU.add))
            v.tensor_scalar(wt_sb, pos_w, -0.5, None, ALU.mult).then_inc(s_w1, 1)
            for m in range(4):
                v.wait_ge(s_gy[m], 64)
                for i in range(4 * m, 4 * m + 4):
                    v.wait_ge(s_at, i + 1)
                    v.tensor_tensor(x1[:, i, :], x1[:, i, :], pg[i % 2][:, 0:C], ALU.add).then_inc(s_a1, 1)
                    v.wait_ge(s_a1, i + 1)
                    step(v, v.scalar_tensor_tensor(out=x1[:, i, :], in0=yg[:, i, :], scalar=top_w[:, i:i + 1],
                                                   in1=x1[:, i, :], op0=ALU.mult, op1=ALU.add))
                    step(v, v.bn_stats(stats[:, i, :], x1[:, i, :]))
                    step(v, v.bn_aggr(mv[:, i, :], stats[:, i, :]))
                v.tensor_scalar(ve[:, 4 * m:4 * m + 4], mv[:, 4 * m:4 * m + 4, 1], EPS, None, ALU.add).then_inc(s_v1, 1)
                v.wait_ge(s_q1, m + 1)
                step(v, v.reciprocal(rstd[:, 4 * m:4 * m + 4], ve[:, 4 * m:4 * m + 4]))
                if m == 0:
                    v.wait_ge(s_zz, 1)
                for i in range(4 * m, 4 * m + 4):
                    b, r = i // 8, 2 * (i % 8)
                    if i >= 4:
                        v.wait_ge(s_xca, 2 * (i - 3))
                        v.wait_ge(s_qt, i - 3)
                    v.tensor_scalar(xln[:, i % 4, :], x1[:, i, :], mv[:, i, 0:1], rstd[:, i:i + 1],
                                    ALU.subtract, ALU.mult).then_inc(s_ln, 1)
                    v.wait_ge(s_ln, i + 1)
                    step(v, v.tensor_scalar(xq[:, i % 4, :], xln[:, i % 4, :], TH_X, None, ALU.is_gt))
                    v.scalar_tensor_tensor(out=xq[:, i % 4, :], in0=xln[:, i % 4, :], scalar=-TH_X,
                                           in1=xq[:, i % 4, :], op0=ALU.is_lt, op1=ALU.subtract).then_inc(s_xq, 1)
                    v.tensor_copy(xc[0:64, b, r, KS - 1:KS - 1 + C], xln[0:64, i % 4, :]).then_inc(s_xcv, 1)
                    v.tensor_copy(xc[64:128, b, r + 1, KS - 2:KS - 2 + C], xln[64:128, i % 4, :]).then_inc(s_xcv, 1)
                if m:
                    for i in range(4 * m - 4, 4 * m):
                        v.wait_ge(s_f, i + 1)
                        v.tensor_tensor(x1[:, i, :], x1[:, i, :], dense_bank[i % 4][:, 0:C], ALU.add).then_inc(s_fa, 1)
            for i in range(NT - 4, NT):
                v.wait_ge(s_f, i + 1)
                v.tensor_tensor(x1[:, i, :], x1[:, i, :], dense_bank[i % 4][:, 0:C], ALU.add).then_inc(s_fa, 1)
            v.wait_ge(s_zz, 2)

            def add_row(r, par, mask, s_done, before_):
                zr = z[:, ds(r, 1), :, :].rearrange("p a b s -> p (a b) s")
                v.wait_ge(s_done, before_)
                for b in range(BATCH):
                    src = (pg if par == 0 else pu)[b][:, 0:SPAN]
                    if mask is None:
                        ins = v.tensor_tensor(zr[:, b, :], zr[:, b, :], src, ALU.add)
                    else:
                        ins = v.scalar_tensor_tensor(out=zr[:, b, :], in0=src, scalar=mask, in1=zr[:, b, :],
                                                     op0=ALU.mult, op1=ALU.add)
                ins.then_inc(s_done, 1)

            v.sem_inc(s_za, 1)
            with v.Fori(0, SLOTS // 2) as it:
                for n in range(2):
                    s = it * 2 + n
                    r = v.value_load(srow_i[0:1, ds(s, 1)], min_val=0, max_val=NROW - 1)
                    v.wait_ge(s_zp, s + 2)
                    add_row(r, n, None, s_za, s + 1)
            many = v.value_load(pairs_i[0:1, 0:1], min_val=0, max_val=NBLK)
            with v.If(many > SLOTS):
                v.wait_ge(s_za, SLOTS + 1)
                v.sem_inc(s_sv, 1)
                with v.Fori(0, NBLK) as n:
                    r = v.value_load(rows_i[0:1, ds(n, 1)], min_val=0, max_val=NROW - 1)
                    v.wait_ge(s_sp, n + 2)
                    add_row(r, 0, spill[:, ds(n, 1)], s_sv, n + 1)
                v.wait_ge(s_sv, NBLK + 1)
            v.wait_ge(s_za, SLOTS + 1)
            v.wait_ge(s_ba, NBLK + 1)
            v.wait_ge(s_fa, NT)
            v.memset(ve[:, 0:1], 0.0).then_inc(s_fz, 1)
            for jj in range(NROW // 2):
                v.wait_ge(s_sh, 2 * jj + 2)
                if jj >= 2:
                    v.wait_ge(s_o[jj % 2], 16 * (jj // 2))
                v.tensor_tensor(res[0:64, jj % 2], z[0:64, 2 * jj, :, 0:C], shifted[0:64, jj % 2], ALU.add)\
                    .then_inc(s_fz, 1)
                v.tensor_tensor(res[64:128, jj % 2], z[64:128, 2 * jj + 1, :, TAPS:TAPS + C],
                                shifted[64:128, jj % 2], ALU.add).then_inc(s_fz, 1)
                v.wait_ge(s_fz, 3 * jj + 3)
                v.tensor_tensor(res[:, jj % 2], res[:, jj % 2], x1[:, jj:NT:NROW // 2, :], ALU.add)\
                    .then_inc(s_fz, 1)


def kernel(**inputs):
    import concourse.bacc as bacc
    from concourse.bass_utils import run_bass_kernel_spmd

    a = {k: np.asarray(v) for k, v in inputs.items()}

    def chunks(v):
        return v.reshape(KC, P).T

    blk = a["L1_attn_block_values"].reshape(NBLK, BS, BS, 2, TAPS // 2, 2)
    arrays = {
        "x": a["L0_attn_x"].reshape(BATCH * SEQ, C),
        "w_rvk": a["L0_attn_W_rvk"].T,
        "w_out": a["L0_attn_W_out"].T,
        "decay": chunks(a["L0_attn_time_decay"]),
        "first": chunks(a["L0_attn_time_first"]),
        "w_r": a["L0_ffn_Wr"],
        "b_r": a["L0_ffn_br"],
        "w_g": a["L0_ffn_Wg"],
        "w_u": a["L0_ffn_Wu"],
        "w_d": a["L0_ffn_Wd"],
        "blocks": blk.transpose(0, 5, 2, 4, 3, 1).reshape(NBLK, P, BW),
        "cols": a["L1_attn_cols"],
        "rows": a["L1_attn_rows"],
        "w_t": a["L1_ffn_weight"].T,
        "rram": a["L1_ffn_rram_variation"].T,
    }
    arrays = {k: np.ascontiguousarray(v) for k, v in arrays.items()}
    nc = bacc.Bacc("TRN2", target_bir_lowering=False, num_devices=1)
    args = {k: nc.dram_tensor(k, v.shape, mybir.dt.from_np(v.dtype), kind="ExternalInput").ap()
            for k, v in arrays.items()}
    out = nc.dram_tensor("out", (BATCH * SEQ, C), F32, kind="ExternalOutput").ap()
    build(nc, out=out, **args)
    r = run_bass_kernel_spmd(nc, [arrays], core_ids=[0])
    return r.results[0]["out"].reshape(BATCH, SEQ, C)
```

```python
from contextlib import ExitStack

import numpy as np

import concourse.bass as bass
from concourse import mybir

F32 = mybir.dt.float32
I32 = mybir.dt.int32
F32R = mybir.dt.float32r
ALU = mybir.AluOpType
ACT = mybir.ActivationFunctionType
AX = mybir.AxisListType
ds = bass.ds

P = 128
BATCH, SEQ, C = 2, 1024, 256
NT = BATCH * SEQ // P
KC = C // P
NE, FF = 4, 1024
KF = FF // P
MT = NT + NE - 1
LOADS = MT + 2
QT = 512
ROUNDS = BATCH * SEQ // QT
NBLK, BS, KS = 128, 64, 16
NROW = SEQ // BS
TAPS = KS // 2
SPAN = C + TAPS
XW = C + KS
SLOTS = 16
BW = KS * BS // 2
RING = 3
TH_X, TH_W, SC_W = 0.33, 0.2, 0.6
EPS = 1e-5
UNIT = 19
RP = 6


def col_of(i):
    b, half, m = i // 8, (i % 8) // 4, i % 4
    return (2 * half + b) * QT + m * P


def build(nc, x, w_rvk, w_out, decay, first, w_r, b_r, w_g, w_u, w_d, blocks, cols, rows, w_t, rram, out):
    x_v = x.rearrange("(i p) c -> p i c", p=P)
    out_v = out.rearrange("(i p) c -> p i c", p=P)
    slots_x = nc.dram_tensor("slots_x", (LOADS * P, C), F32).ap()
    slots_y = nc.dram_tensor("slots_y", (MT * P, C), F32).ap()

    with ExitStack() as ctx:
        place = {}

        def sb(name, shape, dt=F32):
            place[name] = -(-nc.sbuf_base // 32) * 32
            return ctx.enter_context(nc.sbuf_tensor(name, shape, dt))

        def over(name, base, first_col, cols_):
            return nc.alloc_sbuf_tensor_at(name, [P, cols_], F32R, offset=place[base] + 4 * first_col)[:, :]

        def bank(name):
            return ctx.enter_context(nc.psum_tensor(name, [P, 512], F32))

        def sem(name):
            return ctx.enter_context(nc.semaphore(name))

        per_e = 3 * KC * FF
        per_r = 3 * KC * QT
        assert 2 * per_r == per_e and ROUNDS == 4
        big = sb("big", [P, NE * per_e + per_r + 3 * (QT + 1) + 3 * QT])
        up_at, down_at = KC * FF, 2 * KC * FF
        kvr_loop = big[:, (NE - 1) * per_e:NE * per_e + per_r].rearrange("p (j c a t) -> p j c a t",
                                                                       j=ROUNDS - 1, c=KC, a=3)
        kvr0 = sb("kvr0", [P, 1, KC, 3, QT])
        at = 0

        def part(cols_):
            nonlocal at
            at += cols_
            assert at <= NE * per_e
            return big[:, at - cols_:at]

        xc = part(BATCH * NROW * XW).rearrange("p (b r u) -> p b r u", b=BATCH, r=NROW)
        z = part(NROW * BATCH * SPAN).rearrange("p (r b s) -> p r b s", r=NROW, b=BATCH)
        yg_at = at
        yg = part(NT * C).rearrange("p (i c) -> p i c", i=NT)

        tr = sb("tr", [P, KC, NT * P])
        acc = sb("acc", [P, (SLOTS + 1) * BW])
        x_in = acc[:, 0:NT * C].rearrange("p (i c) -> p i c", i=NT)
        xn = acc[:, NT * C:2 * NT * C].rearrange("p (i c) -> p i c", i=NT)
        accs = acc[:, :].rearrange("p (g w) -> p g w", w=BW)
        ring = sb("ring", [P, RING, BW])
        wk = big[:, NE * per_e:]
        opq = wk[:, per_r:per_r + 3 * (QT + 1)].rearrange("p (a t) -> p a t", a=3)
        o0 = per_r + 3 * (QT + 1)
        b1, b2, b3 = (wk[:, o0 + n * QT:o0 + (n + 1) * QT] for n in range(3))
        x1 = wk[:, 0:NT * C].rearrange("p (i c) -> p i c", i=NT)
        o1 = NT * C
        wout_sb = wk[:, o1:o1 + KC * C].rearrange("p (k c) -> p k c", k=KC)
        wt_sb = wk[:, o1 + 512:o1 + 1024].rearrange("p (k c) -> p k c", k=KC)
        rr_sb = wk[:, o1 + 1024:o1 + 1536].rearrange("p (k c) -> p k c", k=KC)
        h = sb("h", [P, FF])
        th = sb("th", [P, 2, 512])
        h_t = sb("h_t", [P, KF, P])
        y_sb = sb("y_sb", [P, 2, C])
        xs = sb("xs", [P, C])
        xs_t = sb("xs_t", [P, 2, KC, P])
        wrvk_sb = sb("wrvk_sb", [P, KC, 3 * C])
        wr_sb = sb("wr_sb", [P, KC, NE])
        br_sb = sb("br_sb", [P, NE])
        dec = sb("dec", [P, KC])
        wv = sb("wv", [P, KC])
        uv = sb("uv", [P, KC])
        carry = sb("carry", [P, KC, ROUNDS + 2, 3])
        ident = sb("ident", [P, P])
        ident_r = sb("ident_r", [P, P], F32R)
        before = sb("before", [P, P])
        after = h[:, 0:P]
        zero = h[:, P:P + C]
        iota = h_t[:, 0, :]
        iota_r = h_t[:, 1, :]
        ones = sb("ones", [P, P])
        starts = sb("starts", [P, NT])
        tiles = sb("tiles", [P, LOADS])
        rows_i = sb("rows_i", [P, NBLK], I32)
        cols_i = sb("cols_i", [P, NBLK], I32)
        rc_i = sb("rc_i", [P, 2], I32)
        slot_i = sb("slot_i", [P, NBLK], I32)
        spill = sb("spill", [P, NBLK])
        srow_i = sb("srow_i", [P, SLOTS], I32)
        scol_i = sb("scol_i", [P, SLOTS], I32)
        pairs_i = sb("pairs_i", [P, 1], I32)
        pos_i = sb("pos_i", [P, NT], I32)
        eid_i = sb("eid_i", [P, LOADS], I32)
        top_w = sb("top_w", [P, NT])
        stats = sb("stats", [P, NT, 6])
        mv = sb("mv", [P, NT, 2])
        ve = sb("ve", [P, NT])
        rstd = sb("rstd", [P, NT])
        nmr = sb("nmr", [P, NT])
        xq_r = over("xq_r", "big", yg_at, NT * C).rearrange("p (i c) -> p i c", i=NT)
        xqt_r = over("xqt_r", "tr", 0, NT * C).rearrange("p (k n) -> p k n", k=KC)
        wt_hi = over("wt_hi", "big", NE * per_e + o1 + 512, KC * C).rearrange("p (k c) -> p k c", k=KC)
        wt_lo = over("wt_lo", "th", 512, KC * C).rearrange("p (k c) -> p k c", k=KC)
        lg = b1[:, 0:64].rearrange("p (i e) -> p i e", e=NE)
        mx = b1[:, 64:80]
        oh = b1[:, 80:144].rearrange("p (i e) -> p i e", e=NE)
        eq = b1[:, 144:208].rearrange("p (i e) -> p i e", e=NE)
        seen = b1[:, 208:224]
        ex = b1[:, 224:288].rearrange("p (i e) -> p i e", e=NE)
        sums = b1[:, 288:304]
        incl = b1[:, 304:368].rearrange("p (e i) -> p e i", e=NE)
        cmp = b1[:, 368:432].rearrange("p (e i) -> p e i", e=NE)
        t_e = b1[:, 432:436]
        t_end = b1[:, 436:440]
        t_beg = b1[:, 440:444]
        ps = b1[:, 444:508].rearrange("p (i e) -> p i e", e=NE)
        pos = b2[:, 0:16]
        ecmp = b2[:, 16:16 + 3 * LOADS].rearrange("p (s e) -> p s e", e=3)
        eid = b2[:, 80:80 + LOADS]
        key = b2[:, 128:256]
        same = b2[:, 256:384]
        tmp = b2[:, 384:512]
        first_b = b3[:, 0:128]
        gid_d = b3[:, 128:256]
        row_b = b3[:, 256:384]
        col_b = b3[:, 384:512]
        sel = opq[:, 0, 0:SLOTS]
        sm = opq[:, 1, 0:16]
        keyc, seenc, firstc, fidx, gid, rowf, colf = (sm[:, n:n + 1] for n in range(7))
        wbuf = h[:, :].rearrange("p (n w) -> p n w", n=2)
        spare = th[:, 0, :]
        half_rows = NROW // 2
        shifted = tr[:, :, :].rearrange("p k n -> p (k n)").rearrange("p (n b c) -> p n b c", n=half_rows, b=BATCH)
        res = x1.rearrange("p i c -> p (i c)").rearrange("p (n b c) -> p n b c", n=half_rows, b=BATCH)

        pg = [bank("pg0"), bank("pg1")]
        pu = [bank("pu0"), bank("pu1")]
        pt = [bank("pt0"), bank("pt1")]
        py = bank("py")
        pr = bank("pr")
        four = [pg[0], pu[0], pg[1], pu[1]]
        seven = four + pt + [py]
        eight = seven + [pr]
        dense_bank = [py, pr]
        s_x = [sem(f"s_x{n}") for n in range(4)]
        s_c = sem("s_c")
        s_zf = sem("s_zf")
        s_we = [sem(f"s_we{n}") for n in range(NE)]
        s_wt = sem("s_wt")
        s_k = sem("s_k")
        s_p = sem("s_p")
        s_ve = sem("s_ve")
        s_sd = sem("s_sd")
        s_xn = sem("s_xn")
        s_tp = sem("s_tp")
        s_ta = sem("s_ta")
        s_tv = sem("s_tv")
        s_lg = sem("s_lg")
        s_sub = sem("s_sub")
        s_el = sem("s_el")
        s_oh = sem("s_oh")
        s_cn = sem("s_cn")
        s_pos = sem("s_pos")
        s_fb = sem("s_fb")
        s_gp = sem("s_gp")
        s_gd = sem("s_gd")
        s_gt = sem("s_gt")
        s_cv = sem("s_cv")
        s_sc = sem("s_sc")
        s_bk = [sem(f"s_bk{n}") for n in range(RING)]
        s_ba = sem("s_ba")
        s_xs = sem("s_xs")
        s_xt = sem("s_xt")
        s_xe = sem("s_xe")
        s_gu = sem("s_gu")
        s_th = sem("s_th")
        s_ha = sem("s_ha")
        s_h = sem("s_h")
        s_tr = sem("s_tr")
        s_ht = sem("s_ht")
        s_y = sem("s_y")
        s_ye = sem("s_ye")
        s_ys = [sem("s_ys0"), sem("s_ys1")]
        s_rv = sem("s_rv")
        s_re = sem("s_re")
        s_wk = sem("s_wk")
        s_ex = sem("s_ex")
        s_cu = sem("s_cu")
        s_l1 = sem("s_l1")
        s_gy = [sem(f"s_gy{n}") for n in range(4)]
        s_zz = sem("s_zz")
        s_at = sem("s_at")
        s_e = sem("s_e")
        s_a1 = sem("s_a1")
        s_v1 = sem("s_v1")
        s_q0 = sem("s_q0")
        s_q1 = sem("s_q1")
        s_nm = sem("s_nm")
        s_ln = sem("s_ln")
        s_lo = sem("s_lo")
        s_xq = sem("s_xq")
        s_xca = sem("s_xca")
        s_xcv = sem("s_xcv")
        s_w1 = sem("s_w1")
        s_qt = sem("s_qt")
        s_qe = sem("s_qe")
        s_j = sem("s_j")
        s_f = sem("s_f")
        s_fa = sem("s_fa")
        s_wb = sem("s_wb")
        s_z1 = sem("s_z1")
        s_z0 = sem("s_z0")
        s_zp = sem("s_zp")
        s_za = sem("s_za")
        s_sd2 = sem("s_sd2")
        s_sp = sem("s_sp")
        s_sv = sem("s_sv")
        s_sh = sem("s_sh")
        s_sw = sem("s_sw")
        s_fz = sem("s_fz")
        s_fg = sem("s_fg")
        s_o = sem("s_o")
        block = ctx.enter_context(nc.Block())

        N_CONST = 10
        E3_TURN = 32
        EXPS_AT = (12, 20)
        FIRST_SLOTS = 4
        DENSE_TURN = 4
        N_SMALL = 9

        def stepper(s):
            count = [0]

            def step(eng, ins):
                ins.then_inc(s, 1)
                count[0] += 1
                eng.wait_ge(s, count[0])
            return step

        ROUND_TILES = 4
        TAIL = 1 + ROUND_TILES * (ROUNDS - 1)

        POOL_ROWS = (0, 2, 4)
        VECTOR_ROWS = (6, 7, 1, 3, 5)
        STORE_ORDER = (6, 0, 7, 1, 2, 3, 5, 4)

        VECTOR_SHIFTS = (6, 7)

        def shift_halves(copy, jj, s_done):
            copy(shifted[0:64, jj], z[64:128, 2 * jj, :, TAPS:TAPS + C]).then_inc(s_done, 1)
            copy(shifted[64:128, jj], z[0:64, 2 * jj + 1, :, 0:C]).then_inc(s_done, 1)

        def combine(eng, pairs_, s_done):
            for jj in pairs_:
                if jj in VECTOR_SHIFTS:
                    eng.wait_ge(s_sw, 2 * len(VECTOR_SHIFTS))
                else:
                    eng.wait_ge(s_sh, 2 * jj + 2)
                eng.tensor_tensor(res[0:64, jj], z[0:64, 2 * jj, :, 0:C], shifted[0:64, jj], ALU.add)\
                    .then_inc(s_done, 1)
                eng.tensor_tensor(res[64:128, jj], z[64:128, 2 * jj + 1, :, TAPS:TAPS + C],
                                  shifted[64:128, jj], ALU.add).then_inc(s_done, 1)

        @block.sync
        def _(sp):
            for n in range(4):
                sp.dma_start(x_in[:, 4 * n:4 * n + 4, :], x_v[:, 4 * n:4 * n + 4, :]).then_inc(s_x[n], 16)
            sp.wait_ge(s_k, 1)
            sp.wait_ge(s_c, 16 * N_SMALL)
            sp.dma_start(slots_x.rearrange("(i p) c -> p i c", p=P),
                         zero.unsqueeze(1).to_broadcast([P, LOADS, C])).then_inc(s_zf, 16)

            def load_expert(e):
                w = big[:, e * per_e:(e + 1) * per_e]
                sp.dma_start(w[:, 0:up_at].rearrange("p (k f) -> p k f", k=KC),
                             w_g[e].rearrange("(k p) f -> p k f", p=P)).then_inc(s_we[e], 16)
                sp.dma_start(w[:, up_at:down_at].rearrange("p (k f) -> p k f", k=KC),
                             w_u[e].rearrange("(k p) f -> p k f", p=P)).then_inc(s_we[e], 16)
                sp.dma_start(w[:, down_at:].rearrange("p (k c) -> p k c", k=KF),
                             w_d[e].rearrange("(k p) c -> p k c", p=P)).then_inc(s_we[e], 16)

            def expert_here(e):
                sp.wait_ge(s_we[e], 48)
                sp.sem_inc(s_wt, 1)

            load_expert(0)
            sp.wait_ge(s_sc, 16 * NT)
            for n in range(RING):
                sp.dma_start(ring[:, n, :], blocks[n]).then_inc(s_bk[n], 16)
            for e in range(1, NE - 1):
                load_expert(e)
                expert_here(e - 1)
            expert_here(NE - 2)
            full = NBLK // RING

            def refill(n, slot):
                sp.wait_ge(s_ba, n - RING + 2)
                sp.dma_start(ring[:, slot, :], blocks[ds(n, 1)].rearrange("a p w -> p (a w)"))\
                    .then_inc(s_bk[slot], 16)

            def refills(a_, b_):
                with sp.Fori(a_, b_) as i:
                    for n in range(RING):
                        refill(RING * i + n, n)

            refills(1, E3_TURN)
            sp.wait_ge(s_wk, UNIT * KC * (ROUNDS - 1))
            load_expert(NE - 1)
            refills(E3_TURN, E3_TURN + 4)
            expert_here(NE - 1)
            refills(E3_TURN + 4, full)
            for n in range(full * RING, NBLK):
                refill(n, n % RING)
            sp.wait_ge(s_wk, UNIT * 2 * ROUNDS)
            sp.dma_start(wout_sb, w_out.rearrange("(k p) c -> p k c", p=P)).then_inc(s_l1, 16)
            sp.dma_start(x1, x_v).then_inc(s_l1, 16)
            sp.dma_start(wt_sb, w_t.rearrange("(k p) c -> p k c", p=P)).then_inc(s_l1, 16)
            sp.dma_start(rr_sb, rram.rearrange("(k p) c -> p k c", p=P)).then_inc(s_l1, 16)
            sp.wait_ge(s_cv, 1)
            many = sp.value_load(pairs_i[0:1, 0:1], min_val=0, max_val=NBLK)
            with sp.If(many > SLOTS):
                sp.wait_ge(s_zp, SLOTS + 2)
                sp.wait_ge(s_ht, 2 * MT)
                with sp.Fori(0, NBLK) as n:
                    sp.wait_ge(s_sp, n + 1)
                    sp.dma_start(spare, blocks[ds(n, 1)].rearrange("a p w -> p (a w)")).then_inc(s_sd2, 16)
            done = [0, 0]
            for jj in STORE_ORDER:
                own = int(jj in POOL_ROWS)
                done[own] += 2
                if own:
                    sp.wait_ge(s_fg, done[1])
                else:
                    sp.wait_ge(s_fz, done[0] + 1)
                sp.dma_start(out_v[:, jj:NT:NROW // 2, :], res[:, jj]).then_inc(s_o, 16)
            sp.wait_ge(s_o, 16 * (NROW // 2))

        @block.gpsimd
        def _(g):
            step = stepper(s_k)
            step(g, g.memset(zero, 0.0))
            step(g, g.memset(ones[:, :], 1.0))
            step(g, g.memset(ident[:, :], 0.0))
            step(g, g.affine_select(out=ident[:, :], in_=ident[:, :], compare_op=ALU.not_equal, fill=1.0,
                                    base=0, pattern=[[-1, P]], channel_multiplier=1))
            step(g, g.affine_select(out=before[:, :], in_=ones[:, :], compare_op=ALU.is_gt, fill=0.0,
                                    base=0, pattern=[[1, P]], channel_multiplier=-1))
            step(g, g.affine_select(out=after, in_=ones[:, :], compare_op=ALU.is_gt, fill=0.0,
                                    base=0, pattern=[[-1, P]], channel_multiplier=1))
            step(g, g.iota(iota, pattern=[[1, P]], base=0, channel_multiplier=0,
                           allow_small_or_imprecise_dtypes=True))
            step(g, g.iota(iota_r, pattern=[[-1, P]], base=P, channel_multiplier=0,
                           allow_small_or_imprecise_dtypes=True))
            step(g, g.iota(starts[:, :], pattern=[[P, NT]], base=0, channel_multiplier=0,
                           allow_small_or_imprecise_dtypes=True))
            step(g, g.iota(tiles[:, :], pattern=[[1, LOADS]], base=0, channel_multiplier=0,
                           allow_small_or_imprecise_dtypes=True))
            g.wait_ge(s_pos, 1)
            g.wait_ge(s_xn, NT)
            g.wait_ge(s_zf, 16)
            for i in range(NT):
                g.indirect_dma_start(out=slots_x, out_offset=bass.IndirectOffsetOnAxis(ap=pos_i[:, i:i + 1], axis=0),
                                     in_=xn[:, i, :], in_offset=None).then_inc(s_sc, 16)
            g.wait_ge(s_sc, 16 * NT)
            g.wait_ge(s_tp, NT // 2)
            g.memset(acc[:, :], 0.0).then_inc(s_ba, 1)
            g.wait_ge(s_cv, 1)

            def add_block(n, place, turn):
                slot = g.value_load(slot_i[0:1, ds(n, 1)], min_val=0, max_val=SLOTS)
                g.wait_ge(s_bk[place], 16 * turn)
                g.wait_ge(s_ba, n + 1)
                a = accs[:, ds(slot, 1), :].rearrange("p a w -> p (a w)")
                g.tensor_tensor(a, a, ring[:, place, :], ALU.add).then_inc(s_ba, 1)

            with g.Fori(0, NBLK // RING) as i:
                for n in range(RING):
                    add_block(RING * i + n, n, i + 1)
            for n in range(NBLK // RING * RING, NBLK):
                add_block(n, n % RING, n // RING + 1)
            g.wait_ge(s_y, MT)
            for n in range(2):
                g.wait_ge(s_ys[n], 16 * ((MT + 1 - n) // 2 + 1))
            for i in range(NT):
                if i == 4:
                    g.memset(xc[:, :, :, 0:KS], 0.0).then_inc(s_zz, 1)
                g.indirect_dma_start(out=yg[:, i, :], out_offset=None, in_=slots_y,
                                     in_offset=bass.IndirectOffsetOnAxis(ap=pos_i[:, i:i + 1], axis=0))\
                    .then_inc(s_gy[i // 4], 16)
            g.memset(z, 0.0).then_inc(s_zz, 1)
            g.wait_ge(s_fz, 1)
            combine(g, POOL_ROWS, s_fg)

        @block.scalar
        def _(a):
            a.dma_start(wrvk_sb[:, :, :], w_rvk.rearrange("(k p) c -> p k c", p=P)).then_inc(s_c, 16)
            a.dma_start(wr_sb[:, :, :], w_r.rearrange("(k p) e -> p k e", p=P)).then_inc(s_c, 16)
            a.dma_start(br_sb[:, :], b_r.partition_broadcast(P)).then_inc(s_c, 16)
            a.dma_start(dec[:, :], decay).then_inc(s_c, 16)
            a.dma_start(uv[:, :], first).then_inc(s_c, 16)
            a.dma_start(rows_i[:, :], rows.partition_broadcast(P)).then_inc(s_c, 16)
            a.dma_start(cols_i[:, :], cols.partition_broadcast(P)).then_inc(s_c, 16)
            a.dma_start(rc_i[:, 0:1], rows.unsqueeze(1)).then_inc(s_c, 16)
            a.dma_start(rc_i[:, 1:2], cols.unsqueeze(1)).then_inc(s_c, 16)
            a.wait_ge(s_ve, 1)
            a.activation(ve[:, :], ve[:, :], ACT.Sqrt).then_inc(s_sd, 1)
            for n in range(0, NT // 2, 2):
                a.wait_ge(s_tp, n + 1)
                a.activation(tr[:, :, col_of(2 * n):col_of(2 * n) + 2 * P].rearrange("p k (t n) -> p k t n", t=2),
                             four[n % 4][:, :].rearrange("p (t k n) -> p k t n", t=2, k=KC), ACT.Copy)\
                    .then_inc(s_ta, 1)
            a.wait_ge(s_c, 16 * N_SMALL)
            a.activation(wv[:, :], dec[:, :], ACT.Exp).then_inc(s_cu, 1)

            def piece(j, p, src):
                c, kind = p // 3, p % 3
                a.wait_ge(s_rv, RP * j + p + 1)
                dst = (kvr_loop[:, j - 1] if j else kvr0[:, 0])[:, c, kind, :]
                if kind == 2:
                    a.activation(dst, src[:, :], ACT.Tanh, scale=0.5).then_inc(s_re, 1)
                else:
                    a.activation(dst, src[:, :], ACT.Copy).then_inc(s_re, 1)

            def exps(n, c):
                for m, (buf, bias, at_) in enumerate([(b2, None, 4), (b1, uv, 5), (b3, wv, 6),
                                                     (opq[:, 2, 1:QT + 1], None, 7)]):
                    a.wait_ge(s_wk, UNIT * n + at_)
                    if bias is None:
                        a.activation(buf, buf, ACT.Exp).then_inc(s_ex, 1)
                    else:
                        a.activation(buf, buf, ACT.Exp, bias=bias[:, c:c + 1]).then_inc(s_ex, 1)

            def load_slot_tile(s):
                a.dma_start(xs[:, :], slots_x[ds(s * P, P), :]).then_inc(s_xs, 16)

            def slot_tile_out(s, par):
                a.wait_ge(s_xt, s + 1)
                a.activation(xs_t[:, par, :, :], pr[:, 0:KC * P].rearrange("p (k n) -> p k n", k=KC), ACT.Copy)\
                    .then_inc(s_xe, 1)
                load_slot_tile(s + 1)

            def half_t(s, f):
                a.wait_ge(s_tr, 2 * s + f + 1)
                a.activation(h_t[:, 4 * f:4 * f + 4, :], pt[f][:, :].rearrange("p (k n) -> p k n", k=4), ACT.Copy)\
                    .then_inc(s_ht, 1)

            def tanh(s, f):
                a.wait_ge(s_gu, 2 * s + f + 1)
                a.activation(th[:, f, :], pg[f][:, :], ACT.Tanh, scale=0.5).then_inc(s_th, 1)

            def y_out(s, par, reuse):
                a.wait_ge(s_y, s + 1)
                a.wait_ge(s_ys[par], reuse + 16)
                a.activation(y_sb[:, par, :], py[:, 0:C], ACT.Copy).then_inc(s_ye, 1)
                a.wait_ge(s_ye, s + 1)
                a.dma_start(slots_y[ds(s * P, P), :], y_sb[:, par, :]).then_inc(s_ys[par], 16)

            def tile(s, par, unit=None, first_tile=False, stored=None):
                tanh(s, 0)
                if not first_tile:
                    half_t(s - 1, 1)
                slot_tile_out(s + 1, 1 - par)
                tanh(s, 1)
                if not first_tile:
                    y_out(s - 1, 1 - par, stored)
                half_t(s, 0)
                if unit:
                    exps(*unit)

            for n in range(2):
                a.sem_inc(s_ys[n], 16)
            for q in range(RP * ROUNDS):
                if q == 1:
                    a.wait_ge(s_sub, 1)
                    a.activation(ex, lg, ACT.Exp).then_inc(s_el, 1)
                if q in EXPS_AT:
                    exps(EXPS_AT.index(q), EXPS_AT.index(q) % KC)
                piece(q // RP, q % RP, seven[q % 7])
            a.wait_ge(s_sc, 16 * NT)
            load_slot_tile(0)
            slot_tile_out(0, 0)
            tile(0, 0, first_tile=True)
            with a.Fori(0, ROUNDS - 1) as it:
                for jj in range(ROUND_TILES):
                    unit = (it * 2 + (2 + jj // 2), jj // 2) if jj % 2 == 0 else None
                    tile(it * ROUND_TILES + (1 + jj), (1 + jj) % 2, unit, stored=(it * 2 + (jj // 2)) * 16)
            with a.Fori(0, (MT - TAIL) // 2) as it:
                for jj in range(2):
                    tile(it * 2 + (TAIL + jj), (TAIL + jj) % 2, stored=(it + (TAIL + jj - 1) // 2) * 16)
            half_t(MT - 1, 1)
            y_out(MT - 1, (MT - 1) % 2, ((MT - 1) // 2) * 16)
            a.activation(ve[:, 0:1], ve[:, 0:1], ACT.Sqrt).then_inc(s_q0, 1)

            def root(m):
                a.wait_ge(s_v1, m + 1)
                a.activation(ve[:, 4 * m:4 * m + 4], ve[:, 4 * m:4 * m + 4], ACT.Sqrt).then_inc(s_q1, 1)

            def normalise(i):
                b, r = i // 8, 2 * (i % 8)
                a.activation(xc[64:128, b, r + 1, KS - 2:KS - 2 + C], x1[64:128, i, :], ACT.Identity,
                             bias=nmr[64:128, i:i + 1], scale=rstd[64:128, i:i + 1]).then_inc(s_lo, 1)

            def shift(i):
                b, r = i // 8, 2 * (i % 8)
                a.wait_ge(s_lo, i + 1)
                a.activation(xc[0:64, b, r + 1, KS - 1:KS - 1 + C], xc[64:128, b, r + 1, KS - 2:KS - 2 + C], ACT.Copy)\
                    .then_inc(s_xca, 1)
                a.wait_ge(s_ln, i + 1)
                a.activation(xc[64:128, b, r, KS - 2:KS - 2 + C], xc[0:64, b, r, KS - 1:KS - 1 + C], ACT.Copy)\
                    .then_inc(s_xca, 1)

            a.wait_ge(s_zz, 1)
            for m in range(4):
                root(m)
                a.wait_ge(s_nm, m + 1)
                for i in range(4 * m, 4 * m + 4):
                    normalise(i)
                for i in range(4 * m, 4 * m + 4):
                    shift(i)
            a.wait_ge(s_ba, NBLK + 1)

            def weights(it):
                for n in range(2):
                    a.wait_ge(s_zp, it * 2 + (n + 1))
                    a.activation(wbuf[:, n, :], accs[:, ds(it * 2 + n, 1), :].rearrange("p a w -> p (a w)"), ACT.Copy)\
                        .then_inc(s_wb, 1)

            a.sem_inc(s_wb, FIRST_SLOTS)
            with a.Fori(FIRST_SLOTS // 2, DENSE_TURN) as it:
                weights(it)
            for i in range(NT):
                a.wait_ge(s_qt, i + 1)
                a.activation(xqt_r[:, :, col_of(i):col_of(i) + P],
                             pt[i % 2][:, 0:KC * P].rearrange("p (k n) -> p k n", k=KC), ACT.Copy).then_inc(s_qe, 1)
            with a.Fori(DENSE_TURN, SLOTS // 2) as it:
                weights(it)
            a.wait_ge(s_f, NT)
            a.wait_ge(s_za, SLOTS + 2)
            a.wait_ge(s_fz, 1)
            for jj in range(NROW // 2):
                if jj not in VECTOR_SHIFTS:
                    shift_halves(lambda out_, in_: a.activation(out_, in_, ACT.Copy), jj, s_sh)

        @block.tensor
        def _(t):
            t.wait_ge(s_k, N_CONST)
            for n in range(NT // 2):
                t.wait_ge(s_xn, 2 * n + 2)
                if n >= 4:
                    if n % 2 == 0:
                        t.wait_ge(s_ta, (n - 4) // 2 + 1)
                    else:
                        t.wait_ge(s_tv, (n - 5) // 2 + 1)
                for tt in range(2):
                    for k in range(KC):
                        q = (tt * KC + k) * P
                        mm = t.transpose(four[n % 4][:, q:q + P], xn[:, 2 * n + tt, k * P:(k + 1) * P], ident[:, :])
                mm.then_inc(s_tp, 1)
            t.wait_ge(s_ta, NT // 4)
            t.wait_ge(s_tv, NT // 4)
            t.wait_ge(s_c, 16 * N_SMALL)
            for i in range(NT):
                for k in range(KC):
                    mm = t.matmul(pr[:, NE * i:NE * i + NE], tr[:, k, col_of(i):col_of(i) + P], wr_sb[:, k, :],
                                  start=(k == 0), stop=(k == KC - 1))
            mm.then_inc(s_lg, 1)

            def piece(j, p, dst):
                c, kind = p // 3, p % 3
                w0 = (2 - kind) * C + c * P
                for k in range(KC):
                    mm = t.matmul(dst[:, :], wrvk_sb[:, k, w0:w0 + P], tr[:, k, ds(j * QT, QT)],
                                  start=(k == 0), stop=(k == KC - 1))
                mm.then_inc(s_rv, 1)

            def pieces(q0, q1):
                for q in range(q0, q1):
                    if q >= 7:
                        t.wait_ge(s_re, q - 6)
                    piece(q // RP, q % RP, seven[q % 7])

            pieces(0, 1)
            t.wait_ge(s_oh, 1)
            t.matmul(pr[:, 64:128], before[:, :], oh.rearrange("p i e -> p (i e)"), start=True, stop=True)
            t.matmul(pr[:, 128:192], ones[:, :], oh.rearrange("p i e -> p (i e)"), start=True, stop=True)\
                .then_inc(s_cn, 1)
            pieces(1, 3)
            t.wait_ge(s_fb, 1)
            t.matmul(pr[:, 0:P], first_b, before[:, :], start=True, stop=True).then_inc(s_gp, 1)
            pieces(3, 4)
            t.wait_ge(s_gd, 1)
            t.matmul(pr[:, 0:P], ones[:, :], gid_d, start=True, stop=True)
            t.matmul(pr[:, 128:128 + SLOTS], row_b, sel, start=True, stop=True)
            t.matmul(pr[:, 144:144 + SLOTS], col_b, sel, start=True, stop=True)
            t.matmul(pr[:, 160:161], first_b, ones[:, 0:1], start=True, stop=True).then_inc(s_gt, 1)
            pieces(4, RP * ROUNDS)

            def gate_up(s, par, f, e):
                for dst, w_at in ((pg[f], 0), (pu[f], up_at)):
                    for k in range(KC):
                        mm = t.matmul(dst[:, :], xs_t[:, par, k, :],
                                      big[:, ds(e * per_e + (w_at + k * FF + 512 * f), 512)],
                                      start=(k == 0), stop=(k == KC - 1))
                mm.then_inc(s_gu, 1)

            def turn_h(s, f):
                t.wait_ge(s_h, 2 * s + f + 1)
                for k in range(4):
                    q = 4 * f + k
                    mm = t.transpose(pt[f][:, k * P:(k + 1) * P], h[:, q * P:(q + 1) * P], ident[:, :])
                mm.then_inc(s_tr, 1)

            def turn_slots(s):
                t.wait_ge(s_xs, 16 * (s + 1))
                for k in range(KC):
                    mm = t.transpose(pr[:, k * P:(k + 1) * P], xs[:, k * P:(k + 1) * P], ident[:, :])
                mm.then_inc(s_xt, 1)

            def down(s):
                e = t.value_load(eid_i[0:1, ds(s, 1)], min_val=0, max_val=NE - 1)
                t.wait_ge(s_ht, 2 * s + 2)
                t.wait_ge(s_ye, s)
                for k in range(KF):
                    mm = t.matmul(py[:, 0:C], h_t[:, k, :], big[:, ds(e * per_e + (down_at + k * C), C)],
                                  start=(k == 0), stop=(k == KF - 1))
                mm.then_inc(s_y, 1)

            def tile(s, par, first_tile=False):
                e = t.value_load(eid_i[0:1, ds(s, 1)], min_val=0, max_val=NE - 1)
                t.wait_ge(s_wt, e + 1)
                t.wait_ge(s_xe, s + 1)
                if not first_tile:
                    t.wait_ge(s_h, 2 * s - 1)
                gate_up(s, par, 0, e)
                if not first_tile:
                    turn_h(s - 1, 1)
                turn_slots(s + 1)
                if not first_tile:
                    t.wait_ge(s_h, 2 * s)
                gate_up(s, par, 1, e)
                if not first_tile:
                    down(s - 1)
                turn_h(s, 0)

            t.wait_ge(s_pos, 1)
            t.wait_ge(s_re, RP * ROUNDS)
            t.wait_ge(s_cv, 1)
            turn_slots(0)
            t.wait_ge(s_xe, 1)
            tile(0, 0, first_tile=True)
            with t.Fori(0, ROUNDS - 1) as it:
                for jj in range(ROUND_TILES):
                    tile(it * ROUND_TILES + (1 + jj), (1 + jj) % 2)
            with t.Fori(0, (MT - TAIL) // 2) as it:
                for jj in range(2):
                    tile(it * 2 + (TAIL + jj), (TAIL + jj) % 2)
            turn_h(MT - 1, 1)
            down(MT - 1)
            t.wait_ge(s_l1, 64)
            t.wait_ge(s_wk, UNIT * 2 * ROUNDS)

            def attend(i):
                for k in range(KC):
                    mm = t.matmul(eight[i // 2][:, C * (i % 2):C * (i % 2) + C], tr[:, k, col_of(i):col_of(i) + P], wout_sb[:, k, :],
                                  start=(k == 0), stop=(k == KC - 1))
                mm.then_inc(s_at, 1)

            t.wait_ge(s_h, 2 * MT)
            t.wait_ge(s_ye, MT)
            t.wait_ge(s_ht, 2 * MT)
            t.wait_ge(s_xe, MT + 1)
            for i in range(NT):
                attend(i)

            def dense(i):
                t.wait_ge(s_qe, i + 1)
                if i >= 2:
                    t.wait_ge(s_fa, i - 1)
                parts = [(k, w) for k in range(KC) for w in (wt_hi, wt_lo)]
                for n, (k, w) in enumerate(parts):
                    mm = t.matmul(dense_bank[i % 2][:, 0:C], xqt_r[:, k, col_of(i):col_of(i) + P],
                                  w[:, k, :], start=(n == 0), stop=(n == 2 * KC - 1))
                mm.then_inc(s_f, 1)

            t.wait_ge(s_zz, 1)
            t.wait_ge(s_ba, NBLK + 1)
            pz = [(pg[0], pg[1]), (pu[0], pu[1])]

            def conv_one(w, c, b, dst):
                for j in range(TAPS // 2):
                    mm = t.matmul(dst[:, 0:SPAN], w[:, j * P:(j + 1) * P],
                                  xc[:, b, ds(c, 1), 2 * j:2 * j + SPAN].rearrange("p a u -> p (a u)"),
                                  start=(j == 0), stop=(j == TAPS // 2 - 1))
                return mm

            for b in range(BATCH):
                t.wait_ge(s_xca, (b + 1) * NT)
                t.wait_ge(s_ln, (b + 1) * NT // 2)
                t.wait_ge(s_lo, (b + 1) * NT // 2)
                t.wait_ge(s_a1, NT // 4 * (b + 1))
                for s in range(FIRST_SLOTS):
                    c = t.value_load(scol_i[0:1, s:s + 1], min_val=0, max_val=NROW - 1)
                    conv_one(accs[:, s, :], c, b, eight[b * FIRST_SLOTS + s]).then_inc(s_z1, 1)

            def conv(w, c, banks):
                for b in range(BATCH):
                    mm = conv_one(w, c, b, banks[b])
                return mm

            t.sem_inc(s_zp, FIRST_SLOTS + 2)
            def turn(it):
                for n in range(2):
                    s = it * 2 + n
                    c = t.value_load(scol_i[0:1, ds(s, 1)], min_val=0, max_val=NROW - 1)
                    t.wait_ge(s_wb, s + 1)
                    t.wait_ge(s_za, s + 1)
                    conv(wbuf[:, n, :], c, pz[n]).then_inc(s_zp, 1)

            with t.Fori(FIRST_SLOTS // 2, DENSE_TURN) as it:
                turn(it)
            t.wait_ge(s_w1, 1)
            for i in range(NT):
                t.wait_ge(s_xq, 2 * (i // 8) + 2)
                if i >= 2:
                    t.wait_ge(s_qe, i - 1)
                for k in range(KC):
                    mm = t.matmul(pt[i % 2][:, k * P:(k + 1) * P], xq_r[:, i, k * P:(k + 1) * P],
                                  ident_r[:, :], start=True, stop=True)
                mm.then_inc(s_qt, 1)
                if i:
                    dense(i - 1)
            dense(NT - 1)
            with t.Fori(DENSE_TURN, SLOTS // 2) as it:
                turn(it)
            many = t.value_load(pairs_i[0:1, 0:1], min_val=0, max_val=NBLK)
            with t.If(many > SLOTS):
                t.sem_inc(s_sp, 1)
                with t.Fori(0, NBLK) as n:
                    c = t.value_load(cols_i[0:1, ds(n, 1)], min_val=0, max_val=NROW - 1)
                    t.wait_ge(s_sd2, n * 16 + 16)
                    t.wait_ge(s_sv, n + 1)
                    t.wait_ge(s_za, SLOTS + 2)
                    conv(spare, c, pz[0]).then_inc(s_sp, 1)

        @block.vector
        def _(v):
            step = stepper(s_p)
            v.wait_ge(s_k, N_CONST)
            for n in range(4):
                v.wait_ge(s_x[n], 16)
                for i in range(4 * n, 4 * n + 4):
                    ins = v.bn_stats(stats[:, i, :], x_in[:, i, :])
            step(v, ins)
            for i in range(NT):
                ins = v.bn_aggr(mv[:, i, :], stats[:, i, :])
            step(v, ins)
            v.tensor_scalar(ve[:, :], mv[:, :, 1], EPS, None, ALU.add).then_inc(s_ve, 1)
            v.wait_ge(s_sd, 1)
            step(v, v.reciprocal(rstd[:, :], ve[:, :]))
            for i in range(NT):
                v.tensor_scalar(xn[:, i, :], x_in[:, i, :], mv[:, i, 0:1], rstd[:, i:i + 1], ALU.subtract, ALU.mult)\
                    .then_inc(s_xn, 1)
            for n in range(1, NT // 2, 2):
                v.wait_ge(s_tp, n + 1)
                v.tensor_copy(tr[:, :, col_of(2 * n):col_of(2 * n) + 2 * P].rearrange("p k (t n) -> p k t n", t=2),
                              four[n % 4][:, :].rearrange("p (t k n) -> p k t n", t=2, k=KC)).then_inc(s_tv, 1)
            v.wait_ge(s_c, 16 * N_SMALL)
            v.wait_ge(s_lg, 1)
            step(v, v.tensor_tensor(lg, pr[:, 0:64].rearrange("p (i e) -> p i e", e=NE),
                                    br_sb[:, :].unsqueeze(1).to_broadcast([P, NT, NE]), ALU.add))
            step(v, v.tensor_reduce(mx, lg, AX.X, ALU.max))
            v.tensor_tensor(lg, lg, mx.unsqueeze(2).to_broadcast([P, NT, NE]), ALU.subtract).then_inc(s_sub, 1)
            v.wait_ge(s_sub, 1)
            step(v, v.tensor_scalar(eq, lg, 0.0, None, ALU.is_ge))
            step(v, v.tensor_copy(oh[:, :, 0], eq[:, :, 0]))
            step(v, v.tensor_copy(seen, eq[:, :, 0]))
            for e in range(1, NE):
                ins = v.tensor_tensor(oh[:, :, e], eq[:, :, e], seen, ALU.is_gt)
                if e < NE - 1:
                    step(v, ins)
                    step(v, v.tensor_tensor(seen, seen, eq[:, :, e], ALU.max))
            ins.then_inc(s_oh, 1)
            v.wait_ge(s_cn, 1)
            total = pr[:, 128:192].rearrange("p (i e) -> p e i", e=NE)
            for e in range(NE):
                ins = v.tensor_tensor_scan(incl[:, e, :], ones[:, 0:NT], total[:, e, :], 0.0, ALU.mult, ALU.add)
            step(v, ins)
            step(v, v.tensor_tensor(cmp, incl[:, :, NT - 1:NT].to_broadcast([P, NE, NT]),
                                    starts[:, :].unsqueeze(1).to_broadcast([P, NE, NT]), ALU.is_gt))
            step(v, v.tensor_reduce(t_e, cmp, AX.X, ALU.add))
            step(v, v.tensor_tensor_scan(t_end, ones[:, 0:NE], t_e, 0.0, ALU.mult, ALU.add))
            step(v, v.tensor_tensor(t_beg, t_end, t_e, ALU.subtract))
            step(v, v.tensor_tensor(ps, incl.rearrange("p e i -> p i e"), pr[:, 64:128].rearrange(
                "p (i e) -> p i e", e=NE), ALU.add))
            step(v, v.tensor_tensor(ps, ps, pr[:, 128:192].rearrange("p (i e) -> p i e", e=NE), ALU.subtract))
            step(v, v.tensor_scalar(t_beg, t_beg, float(P), None, ALU.mult))
            step(v, v.tensor_tensor(ps, ps, t_beg.unsqueeze(1).to_broadcast([P, NT, NE]), ALU.add))
            step(v, v.tensor_tensor(ps, ps, oh, ALU.mult))
            step(v, v.tensor_reduce(pos, ps, AX.X, ALU.add))
            step(v, v.tensor_copy(pos_i[:, :], pos))
            step(v, v.tensor_tensor(ecmp, tiles[:, :].unsqueeze(2).to_broadcast([P, LOADS, 3]),
                                    t_end[:, 0:3].unsqueeze(1).to_broadcast([P, LOADS, 3]), ALU.is_ge))
            step(v, v.tensor_reduce(eid, ecmp, AX.X, ALU.add))
            v.tensor_copy(eid_i[:, :], eid).then_inc(s_pos, 1)
            step(v, v.scalar_tensor_tensor(out=key, in0=rows_i[:, :], scalar=float(NROW), in1=cols_i[:, :],
                                           op0=ALU.mult, op1=ALU.add))
            step(v, v.scalar_tensor_tensor(out=keyc, in0=rc_i[:, 0:1], scalar=float(NROW), in1=rc_i[:, 1:2],
                                           op0=ALU.mult, op1=ALU.add))
            step(v, v.tensor_copy(rowf, rc_i[:, 0:1]))
            step(v, v.tensor_copy(colf, rc_i[:, 1:2]))
            step(v, v.tensor_scalar(same, key, keyc, None, ALU.is_equal))
            step(v, v.tensor_tensor(tmp, same, after, ALU.mult))
            step(v, v.tensor_reduce(seenc, tmp, AX.X, ALU.add))
            step(v, v.tensor_scalar(firstc, seenc, 0.0, None, ALU.is_equal))
            v.tensor_scalar(first_b, ones[:, :], firstc, None, ALU.mult).then_inc(s_fb, 1)
            step(v, v.tensor_tensor(tmp, same, iota_r, ALU.mult))
            step(v, v.tensor_reduce(fidx, tmp, AX.X, ALU.max))
            step(v, v.tensor_scalar(fidx, fidx, -1.0, float(P), ALU.mult, ALU.add))
            step(v, v.tensor_scalar(same, iota, fidx, None, ALU.is_equal))
            v.wait_ge(s_el, 1)
            step(v, v.tensor_reduce(sums, ex, AX.X, ALU.add))
            step(v, v.reciprocal(top_w[:, :], sums))
            v.wait_ge(s_gp, 1)
            step(v, v.tensor_tensor(tmp, same, pr[:, 0:P], ALU.mult))
            step(v, v.tensor_reduce(gid, tmp, AX.X, ALU.add))
            step(v, v.tensor_scalar(gid_d, ident[:, :], gid, None, ALU.mult))
            step(v, v.tensor_scalar(row_b, ones[:, :], rowf, None, ALU.mult))
            step(v, v.tensor_scalar(col_b, ones[:, :], colf, None, ALU.mult))
            v.tensor_scalar(sel, iota[:, 0:SLOTS], gid, firstc, ALU.is_equal, ALU.mult).then_inc(s_gd, 1)
            v.wait_ge(s_gt, 1)
            step(v, v.tensor_scalar(slot_i[:, :], pr[:, 0:P], float(SLOTS), None, ALU.min))
            step(v, v.tensor_scalar(spill[:, :], pr[:, 0:P], float(SLOTS), None, ALU.is_ge))
            step(v, v.tensor_copy(srow_i[:, :], pr[:, 128:128 + SLOTS]))
            step(v, v.tensor_copy(scol_i[:, :], pr[:, 144:144 + SLOTS]))
            v.tensor_copy(pairs_i[:, :], pr[:, 160:161]).then_inc(s_cv, 1)
            step(v, v.tensor_copy(ident_r[:, :], ident[:, :]))
            step(v, v.memset(carry[:, :, :, 0:1], -1e38))
            step(v, v.memset(carry[:, :, :, 1:3], 0.0))
            v.wait_ge(s_cu, 1)
            step(v, v.tensor_scalar(wv[:, :], wv[:, :], -1.0, None, ALU.mult))

            def wkv(n, j, c, part_, j_static=False):
                kvr = kvr0 if j_static else kvr_loop
                jr = 0 if j_static else j - 1
                kk, vv, tt = (kvr[:, ds(jr, 1), c, q, :].rearrange("p a t -> p (a t)") for q in range(3))
                o_old, o_new = opq[:, 0, 0:QT], opq[:, 0, 1:QT + 1]
                p_old, p_new = opq[:, 1, 0:QT], opq[:, 1, 1:QT + 1]
                q_old, q_new = opq[:, 2, 0:QT], opq[:, 2, 1:QT + 1]
                w_b = wv[:, c:c + 1].to_broadcast([P, QT])
                tt_ = v.tensor_tensor
                stt = v.scalar_tensor_tensor
                pieces = RP * j + 3 * c
                steps = [
                    lambda: v.tensor_copy(opq[:, :, 0:1], carry[:, c, ds(j, 1), :].rearrange("p a q -> p q a")),
                    lambda: v.tensor_tensor_scan(o_new, w_b, kk, opq[:, 0, 0:1], ALU.add, ALU.max),
                    lambda: stt(out=b1, in0=kk, scalar=uv[:, c:c + 1], in1=o_old, op0=ALU.add, op1=ALU.max),
                    lambda: tt_(b2, o_old, b1, ALU.subtract),
                    lambda: tt_(b1, kk, b1, ALU.subtract),
                    lambda: tt_(b3, o_old, o_new, ALU.subtract),
                    lambda: tt_(q_new, kk, o_new, ALU.subtract),
                    lambda: tt_(p_new, q_new, vv, ALU.mult),
                    lambda: v.tensor_tensor_scan(p_new, b3, p_new, opq[:, 1, 0:1], ALU.mult, ALU.add),
                    lambda: v.tensor_tensor_scan(q_new, b3, q_new, opq[:, 2, 0:1], ALU.mult, ALU.add),
                    lambda: tt_(b3, b2, p_old, ALU.mult),
                    lambda: tt_(kk, b1, vv, ALU.mult),
                    lambda: tt_(b3, b3, kk, ALU.add),
                    lambda: tt_(b2, b2, q_old, ALU.mult),
                    lambda: tt_(b2, b2, b1, ALU.add),
                    lambda: v.tensor_copy(carry[:, c, ds(j + 2, 1), :].rearrange("p a q -> p q a"),
                                          opq[:, :, QT:QT + 1]),
                    lambda: v.reciprocal(b2, b2),
                    lambda: stt(out=b3, in0=tt, scalar=1.0, in1=b3, op0=ALU.add, op1=ALU.mult),
                    lambda: stt(out=tr[:, c, ds(j * QT, QT)], in0=b3, scalar=0.5, in1=b2, op0=ALU.mult, op1=ALU.mult),
                ]
                assert len(steps) == UNIT
                waits = {1: [(s_re, pieces + 1)],
                         7: [(s_re, pieces + 2), (s_ex, 4 * n + 4)],
                         17: [(s_re, pieces + 3)],
                         18: [(s_rv, RP * j + RP)]}
                for q in range(*part_):
                    for s_, val in waits.get(q, []):
                        v.wait_ge(s_, val)
                    v.wait_ge(s_wk, UNIT * n + q)
                    steps[q]().then_inc(s_wk, 1)

            def act_half(s, f):
                v.wait_ge(s_th, 2 * s + f + 1)
                v.scalar_tensor_tensor(out=th[:, f, :], in0=th[:, f, :], scalar=1.0, in1=pu[f][:, :],
                                       op0=ALU.add, op1=ALU.mult).then_inc(s_ha, 1)
                v.wait_ge(s_ha, 2 * s + f + 1)
                v.scalar_tensor_tensor(out=h[:, 512 * f:512 * f + 512], in0=pg[f][:, :], scalar=0.5,
                                       in1=th[:, f, :], op0=ALU.mult, op1=ALU.mult).then_inc(s_h, 1)

            def tile(s, unit=None, part_a=None, part_b=None):
                act_half(s, 0)
                if unit:
                    wkv(*unit, part_a)
                act_half(s, 1)
                if unit:
                    wkv(*unit, part_b)

            PARTS = [((0, 3), (3, 7)), ((7, 13), (13, UNIT))]
            for c in range(KC):
                wkv(c, 0, c, (0, UNIT), j_static=True)
            tile(0)
            with v.Fori(0, ROUNDS - 1) as it:
                for jj in range(ROUND_TILES):
                    tile(it * ROUND_TILES + (1 + jj), (it * 2 + (2 + jj // 2), it + 1, jj // 2), *PARTS[jj % 2])
            with v.Fori(0, (MT - TAIL) // 2) as it:
                for jj in range(2):
                    tile(it * 2 + (TAIL + jj))
            step = stepper(s_e)
            v.wait_ge(s_l1, 64)
            pos_w, neg_w = th[:, 0, :].rearrange("p (k c) -> p k c", k=KC), th[:, 1, :].rearrange("p (k c) -> p k c", k=KC)
            step(v, v.tensor_scalar(pos_w, wt_sb, TH_W, SC_W, ALU.is_gt, ALU.mult))
            step(v, v.tensor_scalar(neg_w, wt_sb, -TH_W, -SC_W, ALU.is_lt, ALU.mult))
            step(v, v.tensor_tensor(pos_w, pos_w, neg_w, ALU.add))
            step(v, v.tensor_tensor(pos_w, pos_w, rr_sb, ALU.add))
            step(v, v.tensor_scalar(wt_hi, pos_w, -0.5, None, ALU.mult))
            v.scalar_tensor_tensor(out=wt_lo, in0=pos_w, scalar=-0.5, in1=wt_hi.bitcast(F32), op0=ALU.mult,
                                   op1=ALU.subtract).then_inc(s_w1, 1)

            def attended(m):
                for n in range(2 * m, 2 * m + 2):
                    v.wait_ge(s_at, 2 * n + 2)
                    two = x1[:, 2 * n:2 * n + 2, :].rearrange("p i c -> p (i c)")
                    v.tensor_tensor(two, two, eight[n][:, :], ALU.add).then_inc(s_a1, 1)

            v.wait_ge(s_q0, 1)

            def sums_of(m):
                v.wait_ge(s_gy[m], 64)
                v.wait_ge(s_a1, 2 * m + 2)
                own = range(4 * m, 4 * m + 4)
                for i in own:
                    ins = v.scalar_tensor_tensor(out=x1[:, i, :], in0=yg[:, i, :], scalar=top_w[:, i:i + 1],
                                                 in1=x1[:, i, :], op0=ALU.mult, op1=ALU.add)
                step(v, ins)
                for i in own:
                    ins = v.bn_stats(stats[:, i, :], x1[:, i, :])
                step(v, ins)
                for i in own:
                    ins = v.bn_aggr(mv[:, i, :], stats[:, i, :])
                step(v, ins)
                v.tensor_scalar(ve[:, 4 * m:4 * m + 4], mv[:, 4 * m:4 * m + 4, 1], EPS, None, ALU.add).then_inc(s_v1, 1)

            def normalise(m):
                v.wait_ge(s_q1, m + 1)
                own = slice(4 * m, 4 * m + 4)
                step(v, v.reciprocal(rstd[:, own], ve[:, own]))
                v.scalar_tensor_tensor(out=nmr[:, own], in0=mv[:, own, 0], scalar=-1.0, in1=rstd[:, own],
                                       op0=ALU.mult, op1=ALU.mult).then_inc(s_nm, 1)
                for i in range(4 * m, 4 * m + 4):
                    b, r = i // 8, 2 * (i % 8)
                    v.tensor_scalar(xc[0:64, b, r, KS - 1:KS - 1 + C], x1[0:64, i, :], mv[0:64, i, 0:1],
                                    rstd[0:64, i:i + 1], ALU.subtract, ALU.mult).then_inc(s_ln, 1)

            for m in range(2):
                attended(m)
            for m in range(4):
                sums_of(m)
                if m == 0:
                    v.wait_ge(s_zz, 1)
                normalise(m)
                if m < 2:
                    attended(m + 2)
            v.wait_ge(s_ln, NT)

            def quantise(b):
                v.wait_ge(s_lo, 8 * b + 8)
                for q in range(2):
                    rows_ = slice(64 * q, 64 * q + 64)
                    src = xc[rows_, b, q:NROW:2, KS - 1 - q:KS - 1 - q + C]
                    dst = xq_r[rows_, 8 * b:8 * b + 8, :]
                    step(v, v.tensor_scalar(dst, src, TH_X, None, ALU.is_gt))
                    v.scalar_tensor_tensor(out=dst, in0=src, scalar=-TH_X, in1=dst.bitcast(F32), op0=ALU.is_lt,
                                           op1=ALU.subtract).then_inc(s_xq, 1)

            quantise(0)
            v.wait_ge(s_zz, 2)

            def add_row(r, par, mask, s_done, before_):
                zr = z[:, ds(r, 1), :, :].rearrange("p a b s -> p (a b) s")
                v.wait_ge(s_done, before_)
                for b in range(BATCH):
                    src = (pg if par == 0 else pu)[b][:, 0:SPAN]
                    if mask is None:
                        ins = v.tensor_tensor(zr[:, b, :], zr[:, b, :], src, ALU.add)
                    else:
                        ins = v.scalar_tensor_tensor(out=zr[:, b, :], in0=src, scalar=mask, in1=zr[:, b, :],
                                                     op0=ALU.mult, op1=ALU.add)
                ins.then_inc(s_done, 1)

            def turn(it):
                for n in range(2):
                    s = it * 2 + n
                    r = v.value_load(srow_i[0:1, ds(s, 1)], min_val=0, max_val=NROW - 1)
                    v.wait_ge(s_zp, s + 3)
                    add_row(r, n, None, s_za, s + 2)

            for s in range(FIRST_SLOTS):
                r = v.value_load(srow_i[0:1, s:s + 1], min_val=0, max_val=NROW - 1)
                for b in range(BATCH):
                    v.wait_ge(s_z1, b * FIRST_SLOTS + s + 1)
                    if s:
                        v.wait_ge(s_z0, BATCH * s)
                    zr = z[:, ds(r, 1), b, :].rearrange("p a s -> p (a s)")
                    v.tensor_tensor(zr, zr, eight[b * FIRST_SLOTS + s][:, 0:SPAN], ALU.add).then_inc(s_z0, 1)
            v.wait_ge(s_z0, BATCH * FIRST_SLOTS)
            v.sem_inc(s_za, FIRST_SLOTS + 2)
            quantise(1)
            with v.Fori(FIRST_SLOTS // 2, DENSE_TURN) as it:
                turn(it)
            for i in range(NT):
                v.wait_ge(s_f, i + 1)
                v.tensor_tensor(x1[:, i, :], x1[:, i, :], dense_bank[i % 2][:, 0:C], ALU.add).then_inc(s_fa, 1)
            v.wait_ge(s_fa, NT)
            assert SLOTS // 2 == DENSE_TURN + 2 * BATCH
            with v.Fori(0, BATCH) as b:
                for q in range(2):
                    v.wait_ge(s_za, b * 4 + (2 * DENSE_TURN + 2 + 2 * q))
                    rows_ = slice(64 * q, 64 * q + 64)
                    dst = z[rows_, q:NROW:2, ds(b, 1), TAPS * q:TAPS * q + C].rearrange("p r a c -> p r (a c)")
                    v.tensor_tensor(dst, dst, x1[rows_, ds(b * 8, 8), :], ALU.add).then_inc(s_j, 1)
                    v.wait_ge(s_j, b * 2 + (q + 1))
                    turn(b * 2 + (DENSE_TURN + q))
            many = v.value_load(pairs_i[0:1, 0:1], min_val=0, max_val=NBLK)
            with v.If(many > SLOTS):
                v.wait_ge(s_za, SLOTS + 2)
                v.sem_inc(s_sv, 1)
                with v.Fori(0, NBLK) as n:
                    r = v.value_load(rows_i[0:1, ds(n, 1)], min_val=0, max_val=NROW - 1)
                    v.wait_ge(s_sp, n + 2)
                    add_row(r, 0, spill[:, ds(n, 1)], s_sv, n + 1)
                v.wait_ge(s_sv, NBLK + 1)
            v.wait_ge(s_za, SLOTS + 2)
            v.wait_ge(s_j, 2 * BATCH)
            v.wait_ge(s_f, NT)
            v.memset(ve[:, 0:1], 0.0).then_inc(s_fz, 1)
            for jj in VECTOR_SHIFTS:
                shift_halves(v.tensor_copy, jj, s_sw)
            combine(v, VECTOR_ROWS, s_fz)


def kernel(**inputs):
    import concourse.bacc as bacc
    from concourse.bass_utils import run_bass_kernel_spmd

    a = {k: np.asarray(v) for k, v in inputs.items()}

    def chunks(v):
        return v.reshape(KC, P).T

    blk = a["L1_attn_block_values"].reshape(NBLK, BS, BS, 2, TAPS // 2, 2)
    arrays = {
        "x": a["L0_attn_x"].reshape(BATCH * SEQ, C),
        "w_rvk": a["L0_attn_W_rvk"].T,
        "w_out": a["L0_attn_W_out"].T,
        "decay": chunks(a["L0_attn_time_decay"]),
        "first": chunks(a["L0_attn_time_first"]),
        "w_r": a["L0_ffn_Wr"],
        "b_r": a["L0_ffn_br"],
        "w_g": a["L0_ffn_Wg"],
        "w_u": a["L0_ffn_Wu"],
        "w_d": a["L0_ffn_Wd"],
        "blocks": blk.transpose(0, 5, 2, 4, 3, 1).reshape(NBLK, P, BW),
        "cols": a["L1_attn_cols"],
        "rows": a["L1_attn_rows"],
        "w_t": a["L1_ffn_weight"].T,
        "rram": a["L1_ffn_rram_variation"].T,
    }
    arrays = {k: np.ascontiguousarray(v) for k, v in arrays.items()}
    nc = bacc.Bacc("TRN2", target_bir_lowering=False, num_devices=1, dynamic_dma_scratch_size=4096)
    args = {k: nc.dram_tensor(k, v.shape, mybir.dt.from_np(v.dtype), kind="ExternalInput").ap()
            for k, v in arrays.items()}
    out = nc.dram_tensor("out", (BATCH * SEQ, C), F32, kind="ExternalOutput").ap()
    build(nc, out=out, **args)
    r = run_bass_kernel_spmd(nc, [arrays], core_ids=[0])
    return r.results[0]["out"].reshape(BATCH, SEQ, C)
```

```python
from contextlib import ExitStack

import numpy as np

import concourse.bass as bass
from concourse import mybir

F32 = mybir.dt.float32
I32 = mybir.dt.int32
F32R = mybir.dt.float32r
ALU = mybir.AluOpType
ACT = mybir.ActivationFunctionType
AX = mybir.AxisListType
ds = bass.ds

P = 128
BATCH, SEQ, C = 2, 1024, 256
NT = BATCH * SEQ // P
KC = C // P
NE, FF = 4, 1024
KF = FF // P
MT = NT + NE - 1
LOADS = MT + 2
QT = 512
ROUNDS = BATCH * SEQ // QT
NBLK, BS, KS = 128, 64, 16
NROW = SEQ // BS
TAPS = KS // 2
SPAN = C + TAPS
XW = C + KS
SLOTS = 16
BW = KS * BS // 2
RING = 4
TH_X, TH_W, SC_W = 0.33, 0.2, 0.6
EPS = 1e-5
UNIT = 19
RP = 6


def col_of(i):
    b, half, m = i // 8, (i % 8) // 4, i % 4
    return (2 * half + b) * QT + m * P


def build(nc, x, w_rvk, w_out, decay, first, w_r, b_r, w_g, w_u, w_d, blocks, cols, rows, w_t, rram, out):
    x_v = x.rearrange("(i p) c -> p i c", p=P)
    out_v = out.rearrange("(i p) c -> p i c", p=P)
    slots_x = nc.dram_tensor("slots_x", (LOADS * P, C), F32).ap()
    slots_y = nc.dram_tensor("slots_y", (MT * P, C), F32).ap()

    with ExitStack() as ctx:
        place = {}

        def sb(name, shape, dt=F32):
            place[name] = -(-nc.sbuf_base // 32) * 32
            return ctx.enter_context(nc.sbuf_tensor(name, shape, dt))

        def over(name, base, first_col, cols_):
            return nc.alloc_sbuf_tensor_at(name, [P, cols_], F32R, offset=place[base] + 4 * first_col)[:, :]

        def bank(name):
            return ctx.enter_context(nc.psum_tensor(name, [P, 512], F32))

        def sem(name):
            return ctx.enter_context(nc.semaphore(name))

        per_e = 3 * KC * FF
        per_r = 3 * KC * QT
        assert 2 * per_r == per_e and ROUNDS == 4
        big = sb("big", [P, NE * per_e + per_r + 3 * (QT + 1) + 3 * QT])
        up_at, down_at = KC * FF, 2 * KC * FF
        kvr_loop = big[:, (NE - 1) * per_e:NE * per_e + per_r].rearrange("p (j c a t) -> p j c a t",
                                                                       j=ROUNDS - 1, c=KC, a=3)
        kvr0 = sb("kvr0", [P, 1, KC, 3, QT])
        at = 0

        def part(cols_):
            nonlocal at
            at += cols_
            assert at <= NE * per_e
            return big[:, at - cols_:at]

        xc = part(BATCH * NROW * XW).rearrange("p (b r u) -> p b r u", b=BATCH, r=NROW)
        z = part(NROW * BATCH * SPAN).rearrange("p (r b s) -> p r b s", r=NROW, b=BATCH)
        yg_at = at
        yg = part(NT * C).rearrange("p (i c) -> p i c", i=NT)

        tr = sb("tr", [P, KC, NT * P])
        acc = sb("acc", [P, (SLOTS + 1) * BW])
        x_in = acc[:, 0:NT * C].rearrange("p (i c) -> p i c", i=NT)
        xn = acc[:, NT * C:2 * NT * C].rearrange("p (i c) -> p i c", i=NT)
        accs = acc[:, :].rearrange("p (g w) -> p g w", w=BW)
        ring = sb("ring", [P, RING, BW])
        wk = big[:, NE * per_e:]
        opq = wk[:, per_r:per_r + 3 * (QT + 1)].rearrange("p (a t) -> p a t", a=3)
        o0 = per_r + 3 * (QT + 1)
        b1, b2, b3 = (wk[:, o0 + n * QT:o0 + (n + 1) * QT] for n in range(3))
        x1 = wk[:, 0:NT * C].rearrange("p (i c) -> p i c", i=NT)
        o1 = NT * C
        wout_sb = wk[:, o1:o1 + KC * C].rearrange("p (k c) -> p k c", k=KC)
        wt_sb = wk[:, o1 + 512:o1 + 1024].rearrange("p (k c) -> p k c", k=KC)
        rr_sb = wk[:, o1 + 1024:o1 + 1536].rearrange("p (k c) -> p k c", k=KC)
        h = sb("h", [P, FF])
        th = sb("th", [P, 2, 512])
        h_t = sb("h_t", [P, KF, P])
        y_sb = sb("y_sb", [P, 2, C])
        xs = sb("xs", [P, C])
        xs_t = sb("xs_t", [P, 2, KC, P])
        wrvk_sb = sb("wrvk_sb", [P, KC, 3 * C])
        wr_sb = sb("wr_sb", [P, KC, NE])
        br_sb = sb("br_sb", [P, NE])
        dec = sb("dec", [P, KC])
        wv = sb("wv", [P, KC])
        uv = sb("uv", [P, KC])
        carry = sb("carry", [P, KC, ROUNDS + 2, 3])
        ident = sb("ident", [P, P])
        ident_r = sb("ident_r", [P, P], F32R)
        before = sb("before", [P, P])
        after = h[:, 0:P]
        zero = h[:, P:P + C]
        iota = h_t[:, 0, :]
        iota_r = h_t[:, 1, :]
        ones = sb("ones", [P, P])
        fold = sb("fold", [P, NE])
        starts = sb("starts", [P, NT])
        tiles = sb("tiles", [P, LOADS])
        rows_i = sb("rows_i", [P, NBLK], I32)
        cols_i = sb("cols_i", [P, NBLK], I32)
        rc_i = sb("rc_i", [P, 2], I32)
        slot_i = sb("slot_i", [P, NBLK], I32)
        spill = sb("spill", [P, NBLK])
        srow_i = sb("srow_i", [P, SLOTS], I32)
        scol_i = sb("scol_i", [P, SLOTS], I32)
        pairs_i = sb("pairs_i", [P, 1], I32)
        pos_i = sb("pos_i", [P, NT], I32)
        eid_i = sb("eid_i", [P, LOADS], I32)
        used_i = sb("used_i", [P, 1], I32)
        top_w = sb("top_w", [P, NT])
        stats = sb("stats", [P, NT, 6])
        mv = sb("mv", [P, NT, 2])
        ve = sb("ve", [P, NT])
        rstd = sb("rstd", [P, NT])
        nmr = sb("nmr", [P, NT])
        xq_r = over("xq_r", "big", yg_at, NT * C).rearrange("p (i c) -> p i c", i=NT)
        xqt_r = over("xqt_r", "tr", 0, NT * C).rearrange("p (k n) -> p k n", k=KC)
        wt_hi = over("wt_hi", "big", NE * per_e + o1 + 512, KC * C).rearrange("p (k c) -> p k c", k=KC)
        wt_lo = over("wt_lo", "th", 512, KC * C).rearrange("p (k c) -> p k c", k=KC)
        e2 = 2 * per_e
        x_hi = over("x_hi", "tr", 0, NT * P * KC).rearrange("p (k n) -> p k n", k=KC)
        x_lo = over("x_lo", "big", e2, NT * P * KC).rearrange("p (k n) -> p k n", k=KC)
        w_hi = over("w_hi", "big", e2 + NT * P * KC, KC * 3 * C).rearrange("p (k c) -> p k c", k=KC)
        w_lo = over("w_lo", "wrvk_sb", 0, KC * 3 * C).rearrange("p (k c) -> p k c", k=KC)
        wr_2 = over("wr_2", "big", e2 + NT * P * KC + KC * 3 * C, KC * 2 * NE).rearrange("p (k e) -> p k e", k=KC)
        assert NT * P * KC + KC * 3 * C + KC * 2 * NE <= per_e
        lg_t = big[0:2 * NE, 3 * per_e:3 * per_e + NT * P]
        lg = b1[:, 0:64].rearrange("p (i e) -> p i e", e=NE)
        mx = b1[:, 64:80]
        oh = b1[:, 80:144].rearrange("p (i e) -> p i e", e=NE)
        eq = b1[:, 144:208].rearrange("p (i e) -> p i e", e=NE)
        seen = b1[:, 208:224]
        ex = b1[:, 224:288].rearrange("p (i e) -> p i e", e=NE)
        sums = b1[:, 288:304]
        incl = b1[:, 304:368].rearrange("p (e i) -> p e i", e=NE)
        cmp = b1[:, 368:432].rearrange("p (e i) -> p e i", e=NE)
        t_e = b1[:, 432:436]
        t_end = b1[:, 436:440]
        t_beg = b1[:, 440:444]
        ps = b1[:, 444:508].rearrange("p (i e) -> p i e", e=NE)
        pos = b2[:, 0:16]
        ecmp = b2[:, 16:16 + 3 * LOADS].rearrange("p (s e) -> p s e", e=3)
        eid = b2[:, 80:80 + LOADS]
        key = b2[:, 128:256]
        same = b2[:, 256:384]
        tmp = b2[:, 384:512]
        first_b = b3[:, 0:128]
        gid_d = b3[:, 128:256]
        row_b = b3[:, 256:384]
        col_b = b3[:, 384:512]
        sel = opq[:, 0, 0:SLOTS]
        sm = opq[:, 1, 0:16]
        keyc, seenc, firstc, fidx, gid, rowf, colf = (sm[:, n:n + 1] for n in range(7))
        wbuf = h[:, :].rearrange("p (n w) -> p n w", n=2)
        spare = th[:, 0, :]
        half_rows = NROW // 2
        shifted = tr[:, :, :].rearrange("p k n -> p (k n)").rearrange("p (n b c) -> p n b c", n=half_rows, b=BATCH)
        res = x1.rearrange("p i c -> p (i c)").rearrange("p (n b c) -> p n b c", n=half_rows, b=BATCH)

        pg = [bank("pg0"), bank("pg1")]
        pu = [bank("pu0"), bank("pu1")]
        pt = [bank("pt0"), bank("pt1")]
        py = bank("py")
        pr = bank("pr")
        four = [pg[0], pu[0], pg[1], pu[1]]
        seven = pt + [py] + four
        eight = four + pt + [py, pr]
        dense_bank = [py, pr]
        s_x = [sem(f"s_x{n}") for n in range(4)]
        s_c = sem("s_c")
        s_zf = sem("s_zf")
        s_we = [sem(f"s_we{n}") for n in range(NE)]
        s_wt = sem("s_wt")
        s_k = sem("s_k")
        s_p = sem("s_p")
        s_ve = sem("s_ve")
        s_sd = sem("s_sd")
        s_xn = sem("s_xn")
        s_tp = sem("s_tp")
        s_ta = sem("s_ta")
        s_tv = sem("s_tv")
        s_wh = sem("s_wh")
        s_wl = sem("s_wl")
        s_lt = sem("s_lt")
        s_lc = sem("s_lc")
        s_lg = sem("s_lg")
        s_sub = sem("s_sub")
        s_el = sem("s_el")
        s_oh = sem("s_oh")
        s_cn = sem("s_cn")
        s_pos = sem("s_pos")
        s_fb = sem("s_fb")
        s_gp = sem("s_gp")
        s_gd = sem("s_gd")
        s_gt = sem("s_gt")
        s_cv = sem("s_cv")
        s_sc = sem("s_sc")
        s_bk = [sem(f"s_bk{n}") for n in range(RING)]
        s_ba = sem("s_ba")
        s_xs = sem("s_xs")
        s_xt = sem("s_xt")
        s_xe = sem("s_xe")
        s_gu = sem("s_gu")
        s_th = sem("s_th")
        s_ha = sem("s_ha")
        s_h = sem("s_h")
        s_tr = sem("s_tr")
        s_ht = sem("s_ht")
        s_y = sem("s_y")
        s_ye = sem("s_ye")
        s_ys = [sem("s_ys0"), sem("s_ys1")]
        s_rv = sem("s_rv")
        s_re = sem("s_re")
        s_wk = sem("s_wk")
        s_ex = sem("s_ex")
        s_cu = sem("s_cu")
        s_l1 = sem("s_l1")
        s_gy = [sem(f"s_gy{n}") for n in range(4)]
        s_zz = sem("s_zz")
        s_at = sem("s_at")
        s_e = sem("s_e")
        s_a1 = sem("s_a1")
        s_v1 = sem("s_v1")
        s_q0 = sem("s_q0")
        s_q1 = sem("s_q1")
        s_nm = sem("s_nm")
        s_ln = sem("s_ln")
        s_lo = sem("s_lo")
        s_xq = sem("s_xq")
        s_xca = sem("s_xca")
        s_w1 = sem("s_w1")
        s_qt = sem("s_qt")
        s_qe = sem("s_qe")
        s_j = sem("s_j")
        s_f = sem("s_f")
        s_fa = sem("s_fa")
        s_wb = sem("s_wb")
        s_z1 = sem("s_z1")
        s_z0 = sem("s_z0")
        s_zp = sem("s_zp")
        s_za = sem("s_za")
        s_sd2 = sem("s_sd2")
        s_sp = sem("s_sp")
        s_sv = sem("s_sv")
        s_sh = sem("s_sh")
        s_sw = sem("s_sw")
        s_fz = sem("s_fz")
        s_fg = sem("s_fg")
        s_o = sem("s_o")
        block = ctx.enter_context(nc.Block())

        N_CONST = 10
        E3_TURN = 22
        EXPS_AT = 12
        SLOTS_AT = 22
        FIRST_SLOTS = 4
        DENSE_TURN = 4
        N_SMALL = 9

        def stepper(s):
            count = [0]

            def step(eng, ins):
                ins.then_inc(s, 1)
                count[0] += 1
                eng.wait_ge(s, count[0])
            return step

        E3_TILE = 9
        ROUND_TILES = 4
        LOOP = 2
        TAIL = LOOP + ROUND_TILES * (ROUNDS - 1)
        MAYBE = MT - 2

        def rest(eng, tile_, finish):
            used = eng.value_load(used_i[0:1, 0:1], min_val=NT, max_val=MT)

            def from_(s):
                if s == MT:
                    return finish(s - 1)
                with eng.If(used > s):
                    tile_(s)
                    from_(s + 1)
                with eng.If(used < s + 1):
                    finish(s - 1)

            from_(MAYBE)

        def skip_counts(eng, pairs_):
            for s_, now, _ in pairs_:
                eng.wait_ge(s_, now)
            for s_, _, more in pairs_:
                eng.sem_inc(s_, more)

        POOL_ROWS = (0, 2, 4)
        VECTOR_ROWS = (6, 7, 1, 3, 5)
        STORE_ORDER = (6, 0, 7, 1, 2, 3, 5, 4)

        VECTOR_SHIFTS = (6, 7)

        def shift_halves(copy, jj, s_done):
            copy(shifted[0:64, jj], z[64:128, 2 * jj, :, TAPS:TAPS + C]).then_inc(s_done, 1)
            copy(shifted[64:128, jj], z[0:64, 2 * jj + 1, :, 0:C]).then_inc(s_done, 1)

        def combine(eng, pairs_, s_done):
            for jj in pairs_:
                if jj in VECTOR_SHIFTS:
                    eng.wait_ge(s_sw, 2 * len(VECTOR_SHIFTS))
                else:
                    eng.wait_ge(s_sh, 2 * jj + 2)
                eng.tensor_tensor(res[0:64, jj], z[0:64, 2 * jj, :, 0:C], shifted[0:64, jj], ALU.add)\
                    .then_inc(s_done, 1)
                eng.tensor_tensor(res[64:128, jj], z[64:128, 2 * jj + 1, :, TAPS:TAPS + C],
                                  shifted[64:128, jj], ALU.add).then_inc(s_done, 1)

        @block.sync
        def _(sp):
            for n in range(4):
                sp.dma_start(x_in[:, 4 * n:4 * n + 4, :], x_v[:, 4 * n:4 * n + 4, :]).then_inc(s_x[n], 16)
            sp.dma_start(wrvk_sb[:, :, :], w_rvk.rearrange("(k p) c -> p k c", p=P)).then_inc(s_c, 16)
            sp.wait_ge(s_k, 1)
            sp.wait_ge(s_c, 16 * N_SMALL)
            sp.dma_start(slots_x.rearrange("(i p) c -> p i c", p=P),
                         zero.unsqueeze(1).to_broadcast([P, LOADS, C])).then_inc(s_zf, 16)
            sp.dma_start(slots_y[MAYBE * P:MT * P, :].rearrange("(i p) c -> p i c", p=P),
                         zero.unsqueeze(1).to_broadcast([P, MT - MAYBE, C])).then_inc(s_zf, 16)

            def load_expert(e):
                w = big[:, e * per_e:(e + 1) * per_e]
                sp.dma_start(w[:, 0:up_at].rearrange("p (k f) -> p k f", k=KC),
                             w_g[e].rearrange("(k p) f -> p k f", p=P)).then_inc(s_we[e], 16)
                sp.dma_start(w[:, up_at:down_at].rearrange("p (k f) -> p k f", k=KC),
                             w_u[e].rearrange("(k p) f -> p k f", p=P)).then_inc(s_we[e], 16)
                sp.dma_start(w[:, down_at:].rearrange("p (k c) -> p k c", k=KF),
                             w_d[e].rearrange("(k p) c -> p k c", p=P)).then_inc(s_we[e], 16)

            def expert_here(e):
                sp.wait_ge(s_we[e], 48)
                sp.sem_inc(s_wt, 1)

            load_expert(0)
            sp.wait_ge(s_sc, 16 * NT)
            sp.dma_start(xs[:, :], slots_x[0:P, :]).then_inc(s_xs, 16)
            for n in range(RING):
                sp.dma_start(ring[:, n, :], blocks[n]).then_inc(s_bk[n], 16)
            full = NBLK // RING

            def refill(n, slot):
                sp.wait_ge(s_ba, n - RING + 2)
                sp.dma_start(ring[:, slot, :], blocks[ds(n, 1)].rearrange("a p w -> p (a w)"))\
                    .then_inc(s_bk[slot], 16)

            def refills(a_, b_):
                with sp.Fori(a_, b_) as i:
                    for n in range(RING):
                        refill(RING * i + n, n)

            expert_here(0)
            refills(1, 2)
            sp.wait_ge(s_xs, 32)
            load_expert(1)
            refills(2, 5)
            expert_here(1)
            sp.wait_ge(s_rv, RP * ROUNDS)
            load_expert(2)
            refills(5, 8)
            expert_here(2)
            refills(8, E3_TURN)
            sp.wait_ge(s_wk, UNIT * KC * (ROUNDS - 1))
            load_expert(NE - 1)
            refills(E3_TURN, E3_TURN + 3)
            expert_here(NE - 1)
            refills(E3_TURN + 3, full)
            for n in range(full * RING, NBLK):
                refill(n, n % RING)
            sp.wait_ge(s_wk, UNIT * 2 * ROUNDS)
            sp.dma_start(wout_sb, w_out.rearrange("(k p) c -> p k c", p=P)).then_inc(s_l1, 16)
            sp.dma_start(x1, x_v).then_inc(s_l1, 16)
            sp.dma_start(wt_sb, w_t.rearrange("(k p) c -> p k c", p=P)).then_inc(s_l1, 16)
            sp.dma_start(rr_sb, rram.rearrange("(k p) c -> p k c", p=P)).then_inc(s_l1, 16)
            sp.wait_ge(s_cv, 1)
            many = sp.value_load(pairs_i[0:1, 0:1], min_val=0, max_val=NBLK)
            with sp.If(many > SLOTS):
                sp.wait_ge(s_zp, SLOTS + 2)
                sp.wait_ge(s_ht, 2 * MT)
                with sp.Fori(0, NBLK) as n:
                    sp.wait_ge(s_sp, n + 1)
                    sp.dma_start(spare, blocks[ds(n, 1)].rearrange("a p w -> p (a w)")).then_inc(s_sd2, 16)
            done = [0, 0]
            for jj in STORE_ORDER:
                own = int(jj in POOL_ROWS)
                done[own] += 2
                if own:
                    sp.wait_ge(s_fg, done[1])
                else:
                    sp.wait_ge(s_fz, done[0] + 1)
                sp.dma_start(out_v[:, jj:NT:NROW // 2, :], res[:, jj]).then_inc(s_o, 16)
            sp.wait_ge(s_o, 16 * (NROW // 2))

        @block.gpsimd
        def _(g):
            step = stepper(s_k)
            step(g, g.memset(zero, 0.0))
            step(g, g.memset(ones[:, :], 1.0))
            step(g, g.memset(ident[:, :], 0.0))
            step(g, g.affine_select(out=ident[:, :], in_=ident[:, :], compare_op=ALU.not_equal, fill=1.0,
                                    base=0, pattern=[[-1, P]], channel_multiplier=1))
            step(g, g.affine_select(out=before[:, :], in_=ones[:, :], compare_op=ALU.is_gt, fill=0.0,
                                    base=0, pattern=[[1, P]], channel_multiplier=-1))
            step(g, g.affine_select(out=after, in_=ones[:, :], compare_op=ALU.is_gt, fill=0.0,
                                    base=0, pattern=[[-1, P]], channel_multiplier=1))
            step(g, g.iota(iota, pattern=[[1, P]], base=0, channel_multiplier=0,
                           allow_small_or_imprecise_dtypes=True))
            step(g, g.iota(iota_r, pattern=[[-1, P]], base=P, channel_multiplier=0,
                           allow_small_or_imprecise_dtypes=True))
            step(g, g.iota(starts[:, :], pattern=[[P, NT]], base=0, channel_multiplier=0,
                           allow_small_or_imprecise_dtypes=True))
            step(g, g.iota(tiles[:, :], pattern=[[1, LOADS]], base=0, channel_multiplier=0,
                           allow_small_or_imprecise_dtypes=True))
            g.wait_ge(s_wh, 2)
            g.tensor_tensor(wr_2[:, :, NE:], wr_sb[:, :, :], wr_2[:, :, 0:NE].bitcast(F32), ALU.subtract)\
                .then_inc(s_wl, 1)
            g.tensor_tensor(w_lo, wrvk_sb[:, :, :], w_hi.bitcast(F32), ALU.subtract).then_inc(s_wl, 1)
            g.wait_ge(s_pos, 1)
            g.wait_ge(s_xn, NT)
            g.wait_ge(s_zf, 32)
            for i in range(NT):
                g.indirect_dma_start(out=slots_x, out_offset=bass.IndirectOffsetOnAxis(ap=pos_i[:, i:i + 1], axis=0),
                                     in_=xn[:, i, :], in_offset=None).then_inc(s_sc, 16)
            g.wait_ge(s_sc, 16 * NT)
            g.wait_ge(s_tp, NT // 2)
            g.memset(acc[:, :], 0.0).then_inc(s_ba, 1)
            g.wait_ge(s_cv, 1)

            def add_block(n, place, turn):
                slot = g.value_load(slot_i[0:1, ds(n, 1)], min_val=0, max_val=SLOTS)
                g.wait_ge(s_bk[place], 16 * turn)
                g.wait_ge(s_ba, n + 1)
                a = accs[:, ds(slot, 1), :].rearrange("p a w -> p (a w)")
                g.tensor_tensor(a, a, ring[:, place, :], ALU.add).then_inc(s_ba, 1)

            with g.Fori(0, NBLK // RING) as i:
                for n in range(RING):
                    add_block(RING * i + n, n, i + 1)
            for n in range(NBLK // RING * RING, NBLK):
                add_block(n, n % RING, n // RING + 1)
            g.wait_ge(s_y, MT)
            for n in range(2):
                g.wait_ge(s_ys[n], 16 * ((MT + 1 - n) // 2 + 1))
            for i in range(NT):
                if i == 4:
                    g.memset(xc[:, :, :, 0:KS], 0.0).then_inc(s_zz, 1)
                g.indirect_dma_start(out=yg[:, i, :], out_offset=None, in_=slots_y,
                                     in_offset=bass.IndirectOffsetOnAxis(ap=pos_i[:, i:i + 1], axis=0))\
                    .then_inc(s_gy[i // 4], 16)
            g.memset(z, 0.0).then_inc(s_zz, 1)
            g.wait_ge(s_fz, 1)
            combine(g, POOL_ROWS, s_fg)

        @block.scalar
        def _(a):
            a.dma_start(wr_sb[:, :, :], w_r.rearrange("(k p) e -> p k e", p=P)).then_inc(s_c, 16)
            a.dma_start(br_sb[:, :], b_r.partition_broadcast(P)).then_inc(s_c, 16)
            a.dma_start(dec[:, :], decay).then_inc(s_c, 16)
            a.dma_start(uv[:, :], first).then_inc(s_c, 16)
            a.dma_start(rows_i[:, :], rows.partition_broadcast(P)).then_inc(s_c, 16)
            a.dma_start(cols_i[:, :], cols.partition_broadcast(P)).then_inc(s_c, 16)
            a.dma_start(rc_i[:, 0:1], rows.unsqueeze(1)).then_inc(s_c, 16)
            a.dma_start(rc_i[:, 1:2], cols.unsqueeze(1)).then_inc(s_c, 16)
            for m in range(4):
                a.wait_ge(s_ve, m + 1)
                a.activation(ve[:, 4 * m:4 * m + 4], ve[:, 4 * m:4 * m + 4], ACT.Sqrt).then_inc(s_sd, 1)
            a.wait_ge(s_c, 16 * N_SMALL)
            a.activation(wr_2[:, :, 0:NE], wr_sb[:, :, :], ACT.Copy).then_inc(s_wh, 1)
            a.activation(w_hi, wrvk_sb[:, :, :], ACT.Copy).then_inc(s_wh, 1)
            for n in range(NT // 2):
                a.wait_ge(s_tp, n + 1)
                a.activation(x_hi[:, :, col_of(2 * n):col_of(2 * n) + 2 * P].rearrange("p k (t n) -> p k t n", t=2),
                             eight[n][:, :].rearrange("p (t k n) -> p k t n", t=2, k=KC), ACT.Copy)\
                    .then_inc(s_ta, 1)
            for g in range(ROUNDS):
                a.wait_ge(s_lt, g + 1)
                a.activation(lg_t[:, 512 * g:512 * g + 512], four[g][0:2 * NE, :], ACT.Copy).then_inc(s_lc, 1)
            a.activation(wv[:, :], dec[:, :], ACT.Exp).then_inc(s_cu, 1)

            def piece(j, p, src):
                c, kind = p // 3, p % 3
                a.wait_ge(s_rv, RP * j + p + 1)
                dst = (kvr_loop[:, j - 1] if j else kvr0[:, 0])[:, c, kind, :]
                if kind == 2:
                    a.activation(dst, src[:, :], ACT.Tanh, scale=0.5).then_inc(s_re, 1)
                else:
                    a.activation(dst, src[:, :], ACT.Copy).then_inc(s_re, 1)

            def exps(n, c):
                for m, (buf, bias, at_) in enumerate([(b2, None, 4), (b1, uv, 5), (b3, wv, 6),
                                                     (opq[:, 2, 1:QT + 1], None, 7)]):
                    a.wait_ge(s_wk, UNIT * n + at_)
                    if bias is None:
                        a.activation(buf, buf, ACT.Exp).then_inc(s_ex, 1)
                    else:
                        a.activation(buf, buf, ACT.Exp, bias=bias[:, c:c + 1]).then_inc(s_ex, 1)

            def load_slot_tile(s):
                a.dma_start(xs[:, :], slots_x[ds(s * P, P), :]).then_inc(s_xs, 16)

            def slot_tile_out(s, par):
                a.wait_ge(s_xt, s + 1)
                a.activation(xs_t[:, par, :, :], pr[:, 0:KC * P].rearrange("p (k n) -> p k n", k=KC), ACT.Copy)\
                    .then_inc(s_xe, 1)
                load_slot_tile(s + 1)

            def half_t(s, f):
                a.wait_ge(s_tr, 2 * s + f + 1)
                a.activation(h_t[:, 4 * f:4 * f + 4, :], pt[f][:, :].rearrange("p (k n) -> p k n", k=4), ACT.Copy)\
                    .then_inc(s_ht, 1)

            def tanh(s, f):
                a.wait_ge(s_gu, 2 * s + f + 1)
                a.activation(th[:, f, :], pg[f][:, :], ACT.Tanh, scale=0.5).then_inc(s_th, 1)

            def y_out(s, par, reuse):
                a.wait_ge(s_y, s + 1)
                a.wait_ge(s_ys[par], reuse + 16)
                a.activation(y_sb[:, par, :], py[:, 0:C], ACT.Copy).then_inc(s_ye, 1)
                a.wait_ge(s_ye, s + 1)
                a.dma_start(slots_y[ds(s * P, P), :], y_sb[:, par, :]).then_inc(s_ys[par], 16)

            def tile(s, par, unit=None, first_tile=False, stored=None):
                tanh(s, 0)
                if not first_tile:
                    half_t(s - 1, 1)
                slot_tile_out(s + 1, 1 - par)
                tanh(s, 1)
                if not first_tile:
                    y_out(s - 1, 1 - par, stored)
                half_t(s, 0)
                if unit:
                    exps(*unit)

            for n in range(2):
                a.sem_inc(s_ys[n], 16)
            for q in range(RP * ROUNDS):
                if q == 3:
                    a.wait_ge(s_sub, 1)
                    a.activation(ex, lg, ACT.Exp).then_inc(s_el, 1)
                if q == EXPS_AT:
                    exps(0, 0)
                if q == SLOTS_AT:
                    slot_tile_out(0, 0)
                piece(q // RP, q % RP, seven[q % 7])
            def all_tiles(unit):
                tile(0, 0, unit((1, 1)), first_tile=True)
                tile(1, 1, stored=0)
                with a.Fori(0, ROUNDS - 1) as it:
                    for jj in range(ROUND_TILES):
                        u = (it * 2 + (2 + jj // 2), jj // 2) if jj % 2 == 0 else None
                        tile(it * ROUND_TILES + (LOOP + jj), (LOOP + jj) % 2, unit(u),
                             stored=(it * 2 + (LOOP + jj - 1) // 2) * 16)
                for s in range(TAIL, MAYBE):
                    tile(s, s % 2, stored=(s - 1) // 2 * 16)

            a.wait_ge(s_zf, 32)
            a.wait_ge(s_pos, 1)
            e9 = a.value_load(eid_i[0:1, E3_TILE:E3_TILE + 1], min_val=0, max_val=NE - 1)
            with a.If(e9 > NE - 2):
                exps(1, 1)
                with a.Fori(1, ROUNDS) as j:
                    for c in range(KC):
                        exps(j * 2 + c, c)
                all_tiles(lambda u: None)
            with a.If(e9 < NE - 1):
                all_tiles(lambda u: u)

            def finish(s):
                half_t(s, 1)
                y_out(s, s % 2, s // 2 * 16)
                m = MT - 1 - s
                if m:
                    skip_counts(a, [(s_th, 2 * s + 2, 2 * m), (s_xe, s + 2, m), (s_ht, 2 * s + 2, 2 * m),
                                    (s_ye, s + 1, m)])
                    for q in range(s + 1, MT):
                        a.sem_inc(s_ys[q % 2], 16)

            rest(a, lambda s: tile(s, s % 2, stored=(s - 1) // 2 * 16), finish)
            a.activation(ve[:, 0:1], ve[:, 0:1], ACT.Sqrt).then_inc(s_q0, 1)

            def root(m):
                a.wait_ge(s_v1, m + 1)
                a.activation(ve[:, 4 * m:4 * m + 4], ve[:, 4 * m:4 * m + 4], ACT.Sqrt).then_inc(s_q1, 1)

            def normalise(i):
                b, r = i // 8, 2 * (i % 8)
                a.activation(xc[64:128, b, r + 1, KS - 2:KS - 2 + C], x1[64:128, i, :], ACT.Identity,
                             bias=nmr[64:128, i:i + 1], scale=rstd[64:128, i:i + 1]).then_inc(s_lo, 1)

            def shift(i):
                b, r = i // 8, 2 * (i % 8)
                a.wait_ge(s_lo, i + 1)
                a.activation(xc[0:64, b, r + 1, KS - 1:KS - 1 + C], xc[64:128, b, r + 1, KS - 2:KS - 2 + C], ACT.Copy)\
                    .then_inc(s_xca, 1)
                a.wait_ge(s_ln, i + 1)
                a.activation(xc[64:128, b, r, KS - 2:KS - 2 + C], xc[0:64, b, r, KS - 1:KS - 1 + C], ACT.Copy)\
                    .then_inc(s_xca, 1)

            a.wait_ge(s_zz, 1)
            for m in range(4):
                root(m)
                a.wait_ge(s_nm, m + 1)
                for i in range(4 * m, 4 * m + 4):
                    normalise(i)
                for i in range(4 * m, 4 * m + 4):
                    shift(i)
            a.wait_ge(s_ba, NBLK + 1)

            def weights(it):
                for n in range(2):
                    a.wait_ge(s_zp, it * 2 + (n + 1))
                    a.activation(wbuf[:, n, :], accs[:, ds(it * 2 + n, 1), :].rearrange("p a w -> p (a w)"), ACT.Copy)\
                        .then_inc(s_wb, 1)

            a.sem_inc(s_wb, FIRST_SLOTS)
            with a.Fori(FIRST_SLOTS // 2, DENSE_TURN) as it:
                weights(it)
            for i in range(NT):
                a.wait_ge(s_qt, i + 1)
                a.activation(xqt_r[:, :, col_of(i):col_of(i) + P],
                             pt[i % 2][:, 0:KC * P].rearrange("p (k n) -> p k n", k=KC), ACT.Copy).then_inc(s_qe, 1)
            with a.Fori(DENSE_TURN, SLOTS // 2) as it:
                weights(it)
            a.wait_ge(s_f, NT)
            a.wait_ge(s_za, SLOTS + 2)
            a.wait_ge(s_fz, 1)
            for jj in range(NROW // 2):
                if jj not in VECTOR_SHIFTS:
                    shift_halves(lambda out_, in_: a.activation(out_, in_, ACT.Copy), jj, s_sh)

        @block.tensor
        def _(t):
            t.wait_ge(s_k, N_CONST)
            for n in range(NT // 2):
                t.wait_ge(s_xn, 2 * n + 2)
                for tt in range(2):
                    for k in range(KC):
                        q = (tt * KC + k) * P
                        mm = t.transpose(eight[n][:, q:q + P], xn[:, 2 * n + tt, k * P:(k + 1) * P], ident[:, :])
                mm.then_inc(s_tp, 1)
            def piece(j, p, dst):
                c, kind = p // 3, p % 3
                w0 = (2 - kind) * C + c * P
                parts = [(w, src, k) for k in range(KC) for w, src in ((w_hi, x_hi), (w_lo, x_hi), (w_hi, x_lo))]
                for n, (w, src, k) in enumerate(parts):
                    mm = t.matmul(dst[:, :], w[:, k, w0:w0 + P], src[:, k, j * QT:(j + 1) * QT],
                                  start=(n == 0), stop=(n == len(parts) - 1))
                mm.then_inc(s_rv, 1)

            def pieces(q0, q1):
                for q in range(q0, q1):
                    if q >= 7:
                        t.wait_ge(s_re, q - 6)
                    piece(q // RP, q % RP, seven[q % 7])

            t.wait_ge(s_wh, 2)
            t.wait_ge(s_wl, 1)
            chunk_of = (0, 2, 1, 3)
            for g in range(ROUNDS):
                t.wait_ge(s_ta, 2 * g + 2)
                t.wait_ge(s_tv, 2 * g + 2)
                for n, (src, k) in enumerate((src, k) for src in (x_hi, x_lo) for k in range(KC)):
                    mm = t.matmul(four[g][0:2 * NE, :], wr_2[:, k, :], src[:, k, chunk_of[g] * QT:(chunk_of[g] + 1) * QT],
                                  start=(n == 0), stop=(n == 2 * KC - 1))
                mm.then_inc(s_lt, 1)
            t.wait_ge(s_wl, 2)
            pieces(0, 2)
            for g in range(ROUNDS):
                t.wait_ge(s_lc, g + 1)
                for i in range(4 * g, 4 * g + 4):
                    mm = t.matmul(pr[:, NE * i:NE * i + NE], lg_t[:, i * P:(i + 1) * P], fold[0:2 * NE, :],
                                  start=True, stop=True)
            mm.then_inc(s_lg, 1)

            pieces(2, 4)
            t.wait_ge(s_oh, 1)
            t.matmul(pr[:, 64:128], before[:, :], oh.rearrange("p i e -> p (i e)"), start=True, stop=True)
            t.matmul(pr[:, 128:192], ones[:, :], oh.rearrange("p i e -> p (i e)"), start=True, stop=True)\
                .then_inc(s_cn, 1)
            pieces(4, 9)
            t.wait_ge(s_fb, 1)
            t.matmul(pr[:, 0:P], first_b, before[:, :], start=True, stop=True).then_inc(s_gp, 1)
            pieces(9, 12)
            t.wait_ge(s_gd, 1)
            t.matmul(pr[:, 0:P], ones[:, :], gid_d, start=True, stop=True)
            t.matmul(pr[:, 128:128 + SLOTS], row_b, sel, start=True, stop=True)
            t.matmul(pr[:, 144:144 + SLOTS], col_b, sel, start=True, stop=True)
            t.matmul(pr[:, 160:161], first_b, ones[:, 0:1], start=True, stop=True).then_inc(s_gt, 1)
            pieces(12, SLOTS_AT)

            def gate_up(s, par, f, e):
                for dst, w_at in ((pg[f], 0), (pu[f], up_at)):
                    for k in range(KC):
                        mm = t.matmul(dst[:, :], xs_t[:, par, k, :],
                                      big[:, ds(e * per_e + (w_at + k * FF + 512 * f), 512)],
                                      start=(k == 0), stop=(k == KC - 1))
                mm.then_inc(s_gu, 1)

            def turn_h(s, f):
                t.wait_ge(s_h, 2 * s + f + 1)
                for k in range(4):
                    q = 4 * f + k
                    mm = t.transpose(pt[f][:, k * P:(k + 1) * P], h[:, q * P:(q + 1) * P], ident[:, :])
                mm.then_inc(s_tr, 1)

            def turn_slots(s):
                t.wait_ge(s_xs, 16 * (s + 1))
                for k in range(KC):
                    mm = t.transpose(pr[:, k * P:(k + 1) * P], xs[:, k * P:(k + 1) * P], ident[:, :])
                mm.then_inc(s_xt, 1)

            def down(s):
                e = t.value_load(eid_i[0:1, ds(s, 1)], min_val=0, max_val=NE - 1)
                t.wait_ge(s_ht, 2 * s + 2)
                t.wait_ge(s_ye, s)
                for k in range(KF):
                    mm = t.matmul(py[:, 0:C], h_t[:, k, :], big[:, ds(e * per_e + (down_at + k * C), C)],
                                  start=(k == 0), stop=(k == KF - 1))
                mm.then_inc(s_y, 1)

            def tile(s, par, first_tile=False):
                e = t.value_load(eid_i[0:1, ds(s, 1)], min_val=0, max_val=NE - 1)
                t.wait_ge(s_wt, e + 1)
                t.wait_ge(s_xe, s + 1)
                if not first_tile:
                    t.wait_ge(s_h, 2 * s - 1)
                gate_up(s, par, 0, e)
                if not first_tile:
                    turn_h(s - 1, 1)
                turn_slots(s + 1)
                if not first_tile:
                    t.wait_ge(s_h, 2 * s)
                gate_up(s, par, 1, e)
                if first_tile:
                    t.wait_ge(s_re, RP * ROUNDS)
                else:
                    down(s - 1)
                turn_h(s, 0)

            t.wait_ge(s_pos, 1)
            t.wait_ge(s_cv, 1)
            turn_slots(0)
            pieces(SLOTS_AT, RP * ROUNDS)
            t.wait_ge(s_re, RP * ROUNDS - 3)
            tile(0, 0, first_tile=True)
            tile(1, 1)
            with t.Fori(0, ROUNDS - 1) as it:
                for jj in range(ROUND_TILES):
                    tile(it * ROUND_TILES + (LOOP + jj), (LOOP + jj) % 2)
            for s in range(TAIL, MAYBE):
                tile(s, s % 2)

            def finish(s):
                turn_h(s, 1)
                down(s)
                m = MT - 1 - s
                if m:
                    skip_counts(t, [(s_xt, s + 2, m), (s_gu, 2 * s + 2, 2 * m), (s_tr, 2 * s + 2, 2 * m), (s_y, s + 1, m)])

            rest(t, lambda s: tile(s, s % 2), finish)
            t.wait_ge(s_l1, 64)
            t.wait_ge(s_wk, UNIT * 2 * ROUNDS)

            def attend(i):
                t.matmul(eight[i // 2][:, C * (i % 2):C * (i % 2) + C], ident[:, :], x1[:, i, :],
                         start=True, stop=False)
                for k in range(KC):
                    mm = t.matmul(eight[i // 2][:, C * (i % 2):C * (i % 2) + C], tr[:, k, col_of(i):col_of(i) + P], wout_sb[:, k, :],
                                  start=False, stop=(k == KC - 1))
                mm.then_inc(s_at, 1)

            t.wait_ge(s_h, 2 * MT)
            t.wait_ge(s_ye, MT)
            t.wait_ge(s_ht, 2 * MT)
            t.wait_ge(s_xe, MT + 1)
            for i in range(NT):
                attend(i)

            def dense(i):
                t.wait_ge(s_qe, i + 1)
                if i >= 2:
                    t.wait_ge(s_fa, i - 1)
                parts = [(k, w) for k in range(KC) for w in (wt_hi, wt_lo)]
                for n, (k, w) in enumerate(parts):
                    mm = t.matmul(dense_bank[i % 2][:, 0:C], xqt_r[:, k, col_of(i):col_of(i) + P],
                                  w[:, k, :], start=(n == 0), stop=(n == 2 * KC - 1))
                mm.then_inc(s_f, 1)

            t.wait_ge(s_zz, 1)
            t.wait_ge(s_ba, NBLK + 1)
            pz = [(pg[0], pg[1]), (pu[0], pu[1])]

            def conv_one(w, c, b, dst):
                for j in range(TAPS // 2):
                    mm = t.matmul(dst[:, 0:SPAN], w[:, j * P:(j + 1) * P],
                                  xc[:, b, ds(c, 1), 2 * j:2 * j + SPAN].rearrange("p a u -> p (a u)"),
                                  start=(j == 0), stop=(j == TAPS // 2 - 1))
                return mm

            for b in range(BATCH):
                t.wait_ge(s_xca, (b + 1) * NT)
                t.wait_ge(s_ln, (b + 1) * NT // 2)
                t.wait_ge(s_lo, (b + 1) * NT // 2)
                t.wait_ge(s_a1, NT // 2 * (b + 1))
                for s in range(FIRST_SLOTS):
                    c = t.value_load(scol_i[0:1, s:s + 1], min_val=0, max_val=NROW - 1)
                    conv_one(accs[:, s, :], c, b, eight[b * FIRST_SLOTS + s]).then_inc(s_z1, 1)

            def conv(w, c, banks):
                for b in range(BATCH):
                    mm = conv_one(w, c, b, banks[b])
                return mm

            t.sem_inc(s_zp, FIRST_SLOTS + 2)
            def turn(it):
                for n in range(2):
                    s = it * 2 + n
                    c = t.value_load(scol_i[0:1, ds(s, 1)], min_val=0, max_val=NROW - 1)
                    t.wait_ge(s_wb, s + 1)
                    t.wait_ge(s_za, s + 1)
                    conv(wbuf[:, n, :], c, pz[n]).then_inc(s_zp, 1)

            with t.Fori(FIRST_SLOTS // 2, DENSE_TURN) as it:
                turn(it)
            t.wait_ge(s_w1, 1)
            for i in range(NT):
                t.wait_ge(s_xq, 2 * (i // 8) + 2)
                if i >= 2:
                    t.wait_ge(s_qe, i - 1)
                for k in range(KC):
                    mm = t.matmul(pt[i % 2][:, k * P:(k + 1) * P], xq_r[:, i, k * P:(k + 1) * P],
                                  ident_r[:, :], start=True, stop=True)
                mm.then_inc(s_qt, 1)
                if i:
                    dense(i - 1)
            dense(NT - 1)
            with t.Fori(DENSE_TURN, SLOTS // 2) as it:
                turn(it)
            many = t.value_load(pairs_i[0:1, 0:1], min_val=0, max_val=NBLK)
            with t.If(many > SLOTS):
                t.sem_inc(s_sp, 1)
                with t.Fori(0, NBLK) as n:
                    c = t.value_load(cols_i[0:1, ds(n, 1)], min_val=0, max_val=NROW - 1)
                    t.wait_ge(s_sd2, n * 16 + 16)
                    t.wait_ge(s_sv, n + 1)
                    t.wait_ge(s_za, SLOTS + 2)
                    conv(spare, c, pz[0]).then_inc(s_sp, 1)

        @block.vector
        def _(v):
            step = stepper(s_p)
            v.wait_ge(s_k, N_CONST)
            for m in range(5):
                if m < 4:
                    own = range(4 * m, 4 * m + 4)
                    v.wait_ge(s_x[m], 16)
                    for i in own:
                        ins = v.bn_stats(stats[:, i, :], x_in[:, i, :])
                    step(v, ins)
                    for i in own:
                        ins = v.bn_aggr(mv[:, i, :], stats[:, i, :])
                    step(v, ins)
                    v.tensor_scalar(ve[:, 4 * m:4 * m + 4], mv[:, 4 * m:4 * m + 4, 1], EPS, None, ALU.add)\
                        .then_inc(s_ve, 1)
                if m:
                    v.wait_ge(s_sd, m)
                    step(v, v.reciprocal(rstd[:, 4 * m - 4:4 * m], ve[:, 4 * m - 4:4 * m]))
                    for i in range(4 * m - 4, 4 * m):
                        v.tensor_scalar(xn[:, i, :], x_in[:, i, :], mv[:, i, 0:1], rstd[:, i:i + 1],
                                        ALU.subtract, ALU.mult).then_inc(s_xn, 1)
            step(v, v.tensor_tensor(fold[:, :], ident[:, 0:NE], ident[:, NE:2 * NE], ALU.add))
            for n in range(NT // 2):
                v.wait_ge(s_ta, n + 1)
                own = slice(col_of(2 * n), col_of(2 * n) + 2 * P)
                v.tensor_tensor(x_lo[:, :, own].rearrange("p k (t n) -> p k t n", t=2),
                                eight[n][:, :].rearrange("p (t k n) -> p k t n", t=2, k=KC),
                                x_hi[:, :, own].bitcast(F32).rearrange("p k (t n) -> p k t n", t=2),
                                ALU.subtract).then_inc(s_tv, 1)
            v.wait_ge(s_c, 16 * N_SMALL)
            v.wait_ge(s_lg, 1)
            step(v, v.tensor_tensor(lg, pr[:, 0:64].rearrange("p (i e) -> p i e", e=NE),
                                    br_sb[:, :].unsqueeze(1).to_broadcast([P, NT, NE]), ALU.add))
            step(v, v.tensor_reduce(mx, lg, AX.X, ALU.max))
            v.tensor_tensor(lg, lg, mx.unsqueeze(2).to_broadcast([P, NT, NE]), ALU.subtract).then_inc(s_sub, 1)
            v.wait_ge(s_sub, 1)
            step(v, v.tensor_scalar(eq, lg, 0.0, None, ALU.is_ge))
            step(v, v.tensor_copy(oh[:, :, 0], eq[:, :, 0]))
            step(v, v.tensor_copy(seen, eq[:, :, 0]))
            for e in range(1, NE):
                ins = v.tensor_tensor(oh[:, :, e], eq[:, :, e], seen, ALU.is_gt)
                if e < NE - 1:
                    step(v, ins)
                    step(v, v.tensor_tensor(seen, seen, eq[:, :, e], ALU.max))
            ins.then_inc(s_oh, 1)
            v.wait_ge(s_cn, 1)
            total = pr[:, 128:192].rearrange("p (i e) -> p e i", e=NE)
            for e in range(NE):
                ins = v.tensor_tensor_scan(incl[:, e, :], ones[:, 0:NT], total[:, e, :], 0.0, ALU.mult, ALU.add)
            step(v, ins)
            step(v, v.tensor_tensor(cmp, incl[:, :, NT - 1:NT].to_broadcast([P, NE, NT]),
                                    starts[:, :].unsqueeze(1).to_broadcast([P, NE, NT]), ALU.is_gt))
            step(v, v.tensor_reduce(t_e, cmp, AX.X, ALU.add))
            step(v, v.tensor_tensor_scan(t_end, ones[:, 0:NE], t_e, 0.0, ALU.mult, ALU.add))
            step(v, v.tensor_tensor(t_beg, t_end, t_e, ALU.subtract))
            step(v, v.tensor_tensor(ps, incl.rearrange("p e i -> p i e"), pr[:, 64:128].rearrange(
                "p (i e) -> p i e", e=NE), ALU.add))
            step(v, v.tensor_tensor(ps, ps, pr[:, 128:192].rearrange("p (i e) -> p i e", e=NE), ALU.subtract))
            step(v, v.tensor_scalar(t_beg, t_beg, float(P), None, ALU.mult))
            step(v, v.tensor_tensor(ps, ps, t_beg.unsqueeze(1).to_broadcast([P, NT, NE]), ALU.add))
            step(v, v.tensor_tensor(ps, ps, oh, ALU.mult))
            step(v, v.tensor_reduce(pos, ps, AX.X, ALU.add))
            step(v, v.tensor_copy(pos_i[:, :], pos))
            step(v, v.tensor_copy(used_i[:, :], t_end[:, NE - 1:NE]))
            step(v, v.tensor_tensor(ecmp, tiles[:, :].unsqueeze(2).to_broadcast([P, LOADS, 3]),
                                    t_end[:, 0:3].unsqueeze(1).to_broadcast([P, LOADS, 3]), ALU.is_ge))
            step(v, v.tensor_reduce(eid, ecmp, AX.X, ALU.add))
            v.tensor_copy(eid_i[:, :], eid).then_inc(s_pos, 1)
            step(v, v.scalar_tensor_tensor(out=key, in0=rows_i[:, :], scalar=float(NROW), in1=cols_i[:, :],
                                           op0=ALU.mult, op1=ALU.add))
            step(v, v.scalar_tensor_tensor(out=keyc, in0=rc_i[:, 0:1], scalar=float(NROW), in1=rc_i[:, 1:2],
                                           op0=ALU.mult, op1=ALU.add))
            step(v, v.tensor_copy(rowf, rc_i[:, 0:1]))
            step(v, v.tensor_copy(colf, rc_i[:, 1:2]))
            step(v, v.tensor_scalar(same, key, keyc, None, ALU.is_equal))
            step(v, v.tensor_tensor(tmp, same, after, ALU.mult))
            step(v, v.tensor_reduce(seenc, tmp, AX.X, ALU.add))
            step(v, v.tensor_scalar(firstc, seenc, 0.0, None, ALU.is_equal))
            v.tensor_scalar(first_b, ones[:, :], firstc, None, ALU.mult).then_inc(s_fb, 1)
            step(v, v.tensor_tensor(tmp, same, iota_r, ALU.mult))
            step(v, v.tensor_reduce(fidx, tmp, AX.X, ALU.max))
            step(v, v.tensor_scalar(fidx, fidx, -1.0, float(P), ALU.mult, ALU.add))
            step(v, v.tensor_scalar(same, iota, fidx, None, ALU.is_equal))
            v.wait_ge(s_el, 1)
            step(v, v.tensor_reduce(sums, ex, AX.X, ALU.add))
            step(v, v.reciprocal(top_w[:, :], sums))
            v.wait_ge(s_gp, 1)
            step(v, v.tensor_tensor(tmp, same, pr[:, 0:P], ALU.mult))
            step(v, v.tensor_reduce(gid, tmp, AX.X, ALU.add))
            step(v, v.tensor_scalar(gid_d, ident[:, :], gid, None, ALU.mult))
            step(v, v.tensor_scalar(row_b, ones[:, :], rowf, None, ALU.mult))
            step(v, v.tensor_scalar(col_b, ones[:, :], colf, None, ALU.mult))
            v.tensor_scalar(sel, iota[:, 0:SLOTS], gid, firstc, ALU.is_equal, ALU.mult).then_inc(s_gd, 1)
            v.wait_ge(s_gt, 1)
            step(v, v.tensor_scalar(slot_i[:, :], pr[:, 0:P], float(SLOTS), None, ALU.min))
            step(v, v.tensor_scalar(spill[:, :], pr[:, 0:P], float(SLOTS), None, ALU.is_ge))
            step(v, v.tensor_copy(srow_i[:, :], pr[:, 128:128 + SLOTS]))
            step(v, v.tensor_copy(scol_i[:, :], pr[:, 144:144 + SLOTS]))
            v.tensor_copy(pairs_i[:, :], pr[:, 160:161]).then_inc(s_cv, 1)
            step(v, v.tensor_copy(ident_r[:, :], ident[:, :]))
            step(v, v.memset(carry[:, :, :, 0:1], -1e38))
            step(v, v.memset(carry[:, :, :, 1:3], 0.0))
            v.wait_ge(s_cu, 1)
            step(v, v.tensor_scalar(wv[:, :], wv[:, :], -1.0, None, ALU.mult))

            def wkv(n, j, c, part_, j_static=False):
                kvr = kvr0 if j_static else kvr_loop
                jr = 0 if j_static else j - 1
                kk, vv, tt = (kvr[:, ds(jr, 1), c, q, :].rearrange("p a t -> p (a t)") for q in range(3))
                o_old, o_new = opq[:, 0, 0:QT], opq[:, 0, 1:QT + 1]
                p_old, p_new = opq[:, 1, 0:QT], opq[:, 1, 1:QT + 1]
                q_old, q_new = opq[:, 2, 0:QT], opq[:, 2, 1:QT + 1]
                w_b = wv[:, c:c + 1].to_broadcast([P, QT])
                tt_ = v.tensor_tensor
                stt = v.scalar_tensor_tensor
                pieces = RP * j + 3 * c
                steps = [
                    lambda: v.tensor_copy(opq[:, :, 0:1], carry[:, c, ds(j, 1), :].rearrange("p a q -> p q a")),
                    lambda: v.tensor_tensor_scan(o_new, w_b, kk, opq[:, 0, 0:1], ALU.add, ALU.max),
                    lambda: stt(out=b1, in0=kk, scalar=uv[:, c:c + 1], in1=o_old, op0=ALU.add, op1=ALU.max),
                    lambda: tt_(b2, o_old, b1, ALU.subtract),
                    lambda: tt_(b1, kk, b1, ALU.subtract),
                    lambda: tt_(b3, o_old, o_new, ALU.subtract),
                    lambda: tt_(q_new, kk, o_new, ALU.subtract),
                    lambda: tt_(p_new, q_new, vv, ALU.mult),
                    lambda: v.tensor_tensor_scan(p_new, b3, p_new, opq[:, 1, 0:1], ALU.mult, ALU.add),
                    lambda: v.tensor_tensor_scan(q_new, b3, q_new, opq[:, 2, 0:1], ALU.mult, ALU.add),
                    lambda: tt_(b3, b2, p_old, ALU.mult),
                    lambda: tt_(kk, b1, vv, ALU.mult),
                    lambda: tt_(b3, b3, kk, ALU.add),
                    lambda: tt_(b2, b2, q_old, ALU.mult),
                    lambda: tt_(b2, b2, b1, ALU.add),
                    lambda: v.tensor_copy(carry[:, c, ds(j + 2, 1), :].rearrange("p a q -> p q a"),
                                          opq[:, :, QT:QT + 1]),
                    lambda: v.reciprocal(b2, b2),
                    lambda: stt(out=b3, in0=tt, scalar=1.0, in1=b3, op0=ALU.add, op1=ALU.mult),
                    lambda: stt(out=tr[:, c, ds(j * QT, QT)], in0=b3, scalar=0.5, in1=b2, op0=ALU.mult, op1=ALU.mult),
                ]
                assert len(steps) == UNIT
                waits = {1: [(s_re, pieces + 1)],
                         7: [(s_re, pieces + 2), (s_ex, 4 * n + 4)],
                         17: [(s_re, pieces + 3)],
                         18: [(s_rv, RP * j + RP)]}
                for q in range(*part_):
                    for s_, val in waits.get(q, []):
                        v.wait_ge(s_, val)
                    v.wait_ge(s_wk, UNIT * n + q)
                    steps[q]().then_inc(s_wk, 1)

            def act_half(s, f):
                v.wait_ge(s_th, 2 * s + f + 1)
                v.scalar_tensor_tensor(out=th[:, f, :], in0=th[:, f, :], scalar=1.0, in1=pu[f][:, :],
                                       op0=ALU.add, op1=ALU.mult).then_inc(s_ha, 1)
                v.wait_ge(s_ha, 2 * s + f + 1)
                v.scalar_tensor_tensor(out=h[:, 512 * f:512 * f + 512], in0=pg[f][:, :], scalar=0.5,
                                       in1=th[:, f, :], op0=ALU.mult, op1=ALU.mult).then_inc(s_h, 1)

            def tile(s, unit=None, part_a=None, part_b=None, j_static=False):
                act_half(s, 0)
                if unit:
                    wkv(*unit, part_a, j_static)
                act_half(s, 1)
                if unit:
                    wkv(*unit, part_b, j_static)

            PARTS = [((0, 3), (3, 7)), ((7, 13), (13, UNIT))]
            wkv(0, 0, 0, (0, UNIT), j_static=True)

            def all_tiles(unit):
                for s in range(LOOP):
                    tile(s, unit((1, 0, 1)), *PARTS[s], j_static=True)
                with v.Fori(0, ROUNDS - 1) as it:
                    for jj in range(ROUND_TILES):
                        tile(it * ROUND_TILES + (LOOP + jj), unit((it * 2 + (2 + jj // 2), it + 1, jj // 2)), *PARTS[jj % 2])
                for s in range(TAIL, MAYBE):
                    tile(s)

            e9 = v.value_load(eid_i[0:1, E3_TILE:E3_TILE + 1], min_val=0, max_val=NE - 1)
            with v.If(e9 > NE - 2):
                wkv(1, 0, 1, (0, UNIT), j_static=True)
                with v.Fori(1, ROUNDS) as j:
                    for c in range(KC):
                        wkv(j * 2 + c, j, c, (0, UNIT))
                all_tiles(lambda u: None)
            with v.If(e9 < NE - 1):
                all_tiles(lambda u: u)

            def finish(s):
                m = MT - 1 - s
                if m:
                    skip_counts(v, [(s_ha, 2 * s + 2, 2 * m), (s_h, 2 * s + 2, 2 * m)])

            rest(v, tile, finish)
            step = stepper(s_e)
            v.wait_ge(s_l1, 64)
            pos_w, neg_w = th[:, 0, :].rearrange("p (k c) -> p k c", k=KC), th[:, 1, :].rearrange("p (k c) -> p k c", k=KC)
            step(v, v.tensor_scalar(pos_w, wt_sb, TH_W, SC_W, ALU.is_gt, ALU.mult))
            step(v, v.tensor_scalar(neg_w, wt_sb, -TH_W, -SC_W, ALU.is_lt, ALU.mult))
            step(v, v.tensor_tensor(pos_w, pos_w, neg_w, ALU.add))
            step(v, v.tensor_tensor(pos_w, pos_w, rr_sb, ALU.add))
            step(v, v.tensor_scalar(wt_hi, pos_w, -0.5, None, ALU.mult))
            v.scalar_tensor_tensor(out=wt_lo, in0=pos_w, scalar=-0.5, in1=wt_hi.bitcast(F32), op0=ALU.mult,
                                   op1=ALU.subtract).then_inc(s_w1, 1)

            v.wait_ge(s_q0, 1)

            def sums_of(m):
                v.wait_ge(s_gy[m], 64)
                v.wait_ge(s_at, 4 * m + 4)
                own = range(4 * m, 4 * m + 4)
                for i in own:
                    v.scalar_tensor_tensor(out=x1[:, i, :], in0=yg[:, i, :], scalar=top_w[:, i:i + 1],
                                           in1=eight[i // 2][:, C * (i % 2):C * (i % 2) + C],
                                           op0=ALU.mult, op1=ALU.add).then_inc(s_a1, 1)
                v.wait_ge(s_a1, 4 * m + 4)
                for i in own:
                    ins = v.bn_stats(stats[:, i, :], x1[:, i, :])
                step(v, ins)
                for i in own:
                    ins = v.bn_aggr(mv[:, i, :], stats[:, i, :])
                step(v, ins)
                v.tensor_scalar(ve[:, 4 * m:4 * m + 4], mv[:, 4 * m:4 * m + 4, 1], EPS, None, ALU.add).then_inc(s_v1, 1)

            def normalise(m):
                v.wait_ge(s_q1, m + 1)
                own = slice(4 * m, 4 * m + 4)
                step(v, v.reciprocal(rstd[:, own], ve[:, own]))
                v.scalar_tensor_tensor(out=nmr[:, own], in0=mv[:, own, 0], scalar=-1.0, in1=rstd[:, own],
                                       op0=ALU.mult, op1=ALU.mult).then_inc(s_nm, 1)
                for i in range(4 * m, 4 * m + 4):
                    b, r = i // 8, 2 * (i % 8)
                    v.tensor_scalar(xc[0:64, b, r, KS - 1:KS - 1 + C], x1[0:64, i, :], mv[0:64, i, 0:1],
                                    rstd[0:64, i:i + 1], ALU.subtract, ALU.mult).then_inc(s_ln, 1)

            for m in range(4):
                sums_of(m)
                if m == 0:
                    v.wait_ge(s_zz, 1)
                normalise(m)
            v.wait_ge(s_ln, NT)

            def quantise(b):
                v.wait_ge(s_lo, 8 * b + 8)
                for q in range(2):
                    rows_ = slice(64 * q, 64 * q + 64)
                    src = xc[rows_, b, q:NROW:2, KS - 1 - q:KS - 1 - q + C]
                    dst = xq_r[rows_, 8 * b:8 * b + 8, :]
                    step(v, v.tensor_scalar(dst, src, TH_X, None, ALU.is_gt))
                    v.scalar_tensor_tensor(out=dst, in0=src, scalar=-TH_X, in1=dst.bitcast(F32), op0=ALU.is_lt,
                                           op1=ALU.subtract).then_inc(s_xq, 1)

            quantise(0)
            v.wait_ge(s_zz, 2)

            def add_row(r, par, mask, s_done, before_):
                zr = z[:, ds(r, 1), :, :].rearrange("p a b s -> p (a b) s")
                v.wait_ge(s_done, before_)
                for b in range(BATCH):
                    src = (pg if par == 0 else pu)[b][:, 0:SPAN]
                    if mask is None:
                        ins = v.tensor_tensor(zr[:, b, :], zr[:, b, :], src, ALU.add)
                    else:
                        ins = v.scalar_tensor_tensor(out=zr[:, b, :], in0=src, scalar=mask, in1=zr[:, b, :],
                                                     op0=ALU.mult, op1=ALU.add)
                ins.then_inc(s_done, 1)

            def turn(it):
                for n in range(2):
                    s = it * 2 + n
                    r = v.value_load(srow_i[0:1, ds(s, 1)], min_val=0, max_val=NROW - 1)
                    v.wait_ge(s_zp, s + 3)
                    add_row(r, n, None, s_za, s + 2)

            for s in range(FIRST_SLOTS):
                r = v.value_load(srow_i[0:1, s:s + 1], min_val=0, max_val=NROW - 1)
                for b in range(BATCH):
                    v.wait_ge(s_z1, b * FIRST_SLOTS + s + 1)
                    if s:
                        v.wait_ge(s_z0, BATCH * s)
                    zr = z[:, ds(r, 1), b, :].rearrange("p a s -> p (a s)")
                    v.tensor_tensor(zr, zr, eight[b * FIRST_SLOTS + s][:, 0:SPAN], ALU.add).then_inc(s_z0, 1)
            v.wait_ge(s_z0, BATCH * FIRST_SLOTS)
            v.sem_inc(s_za, FIRST_SLOTS + 2)
            quantise(1)
            with v.Fori(FIRST_SLOTS // 2, DENSE_TURN) as it:
                turn(it)
            for i in range(NT):
                v.wait_ge(s_f, i + 1)
                v.tensor_tensor(x1[:, i, :], x1[:, i, :], dense_bank[i % 2][:, 0:C], ALU.add).then_inc(s_fa, 1)
            v.wait_ge(s_fa, NT)
            assert SLOTS // 2 == DENSE_TURN + 2 * BATCH
            with v.Fori(0, BATCH) as b:
                for q in range(2):
                    v.wait_ge(s_za, b * 4 + (2 * DENSE_TURN + 2 + 2 * q))
                    rows_ = slice(64 * q, 64 * q + 64)
                    dst = z[rows_, q:NROW:2, ds(b, 1), TAPS * q:TAPS * q + C].rearrange("p r a c -> p r (a c)")
                    v.tensor_tensor(dst, dst, x1[rows_, ds(b * 8, 8), :], ALU.add).then_inc(s_j, 1)
                    v.wait_ge(s_j, b * 2 + (q + 1))
                    turn(b * 2 + (DENSE_TURN + q))
            many = v.value_load(pairs_i[0:1, 0:1], min_val=0, max_val=NBLK)
            with v.If(many > SLOTS):
                v.wait_ge(s_za, SLOTS + 2)
                v.sem_inc(s_sv, 1)
                with v.Fori(0, NBLK) as n:
                    r = v.value_load(rows_i[0:1, ds(n, 1)], min_val=0, max_val=NROW - 1)
                    v.wait_ge(s_sp, n + 2)
                    add_row(r, 0, spill[:, ds(n, 1)], s_sv, n + 1)
                v.wait_ge(s_sv, NBLK + 1)
            v.wait_ge(s_za, SLOTS + 2)
            v.wait_ge(s_j, 2 * BATCH)
            v.wait_ge(s_f, NT)
            v.memset(ve[:, 0:1], 0.0).then_inc(s_fz, 1)
            for jj in VECTOR_SHIFTS:
                shift_halves(v.tensor_copy, jj, s_sw)
            combine(v, VECTOR_ROWS, s_fz)


def kernel(**inputs):
    import concourse.bacc as bacc
    from concourse.bass_utils import run_bass_kernel_spmd

    a = {k: np.asarray(v) for k, v in inputs.items()}

    def chunks(v):
        return v.reshape(KC, P).T

    blk = a["L1_attn_block_values"].reshape(NBLK, BS, BS, 2, TAPS // 2, 2)
    arrays = {
        "x": a["L0_attn_x"].reshape(BATCH * SEQ, C),
        "w_rvk": a["L0_attn_W_rvk"].T,
        "w_out": a["L0_attn_W_out"].T,
        "decay": chunks(a["L0_attn_time_decay"]),
        "first": chunks(a["L0_attn_time_first"]),
        "w_r": a["L0_ffn_Wr"],
        "b_r": a["L0_ffn_br"],
        "w_g": a["L0_ffn_Wg"],
        "w_u": a["L0_ffn_Wu"],
        "w_d": a["L0_ffn_Wd"],
        "blocks": blk.transpose(0, 5, 2, 4, 3, 1).reshape(NBLK, P, BW),
        "cols": a["L1_attn_cols"],
        "rows": a["L1_attn_rows"],
        "w_t": a["L1_ffn_weight"].T,
        "rram": a["L1_ffn_rram_variation"].T,
    }
    arrays = {k: np.ascontiguousarray(v) for k, v in arrays.items()}
    nc = bacc.Bacc("TRN2", target_bir_lowering=False, num_devices=1, dynamic_dma_scratch_size=4096)
    args = {k: nc.dram_tensor(k, v.shape, mybir.dt.from_np(v.dtype), kind="ExternalInput").ap()
            for k, v in arrays.items()}
    out = nc.dram_tensor("out", (BATCH * SEQ, C), F32, kind="ExternalOutput").ap()
    build(nc, out=out, **args)
    r = run_bass_kernel_spmd(nc, [arrays], core_ids=[0])
    return r.results[0]["out"].reshape(BATCH, SEQ, C)
```
